# Optimizing a Trainium2 kernel written in Bass

```python
import numpy as np
import jax
import jax.numpy as jnp

def _softmax(x, axis=-1):
    return jax.nn.softmax(x, axis=axis)

def _gelu(x):
    return jax.nn.gelu(x, approximate=True)

def _silu(x):
    return jax.nn.silu(x)

def _sigmoid(x):
    return jax.nn.sigmoid(x)

def _layernorm(x, axis=-1, eps=1e-05):
    m = jnp.mean(x, axis=axis, keepdims=True)
    v = jnp.var(x, axis=axis, keepdims=True)
    return (x - m) / jnp.sqrt(v + eps)

def _scatter_add(tgt, idx, src, axis=0):
    return tgt.at[idx].add(src)

def _segment_sum(src, seg, n):
    return jax.ops.segment_sum(src, seg, n)
kernel_name = 'mk_flamingo_gated_d1_seqx_r8_75d11d'

def setup_inputs(seed: int=0):
    np.random.seed(seed)
    _w = jnp.asarray

    def _rec_inputs():
        import jax
        import jax.numpy as jnp
        _rk = jax.random.key(seed)
        x = -0.0002928 + 1 * jax.random.normal(jax.random.fold_in(_rk, 1), (4, 512, 128), jnp.float32)
        _lenS = 512 - jax.random.randint(jax.random.fold_in(_rk, 7), (4,), 0, max(1, 512 // 4) + 1, jnp.int32)
        _lenS2 = 77 - jax.random.randint(jax.random.fold_in(_rk, 8), (4,), 0, max(1, 77 // 4) + 1, jnp.int32)
        _ctx_1024P = jax.random.normal(jax.random.fold_in(_rk, 11), (4, 16, 128), jnp.float32)
        _ctx_1024c = jax.random.dirichlet(jax.random.fold_in(_rk, 511), 0.3 * jnp.ones((16,), jnp.float32), (4, 77))
        _ctx_1024t = jnp.einsum('bsk,bkd->bsd', _ctx_1024c, _ctx_1024P)
        _ctx_1024t = _ctx_1024t * jax.lax.rsqrt(jnp.mean(jnp.square(_ctx_1024t)) + 1e-12) * 0.953939
        ctx_1024 = 4.13588e-05 + 0.999923 * (_ctx_1024t + 0.3 * jax.random.normal(jax.random.fold_in(_rk, 611), (4, 77, 128), jnp.float32))
        _validS = jnp.arange(512)[None, :] < _lenS[:, None]
        _validS2 = jnp.arange(77)[None, :] < _lenS2[:, None]
        _causal = jnp.tril(jnp.ones((512, 512), dtype=bool))
        mask_BxS2_bk0 = jnp.logical_not(jnp.broadcast_to(_validS2[:, :], (4, 77)))
        _g = jax.random.normal(jax.random.fold_in(_rk, 9001), (2, 1), jnp.float32)
        _g = jnp.sign(_g) * jnp.maximum(jnp.abs(_g), 1.0) + (_g == 0) * 1.0
        g_xattn = _g[0]
        g_ffn = _g[1]
        return (x, ctx_1024, mask_BxS2_bk0, g_xattn, g_ffn)
    x, ctx_1024, mask_BxS2_bk0, g_xattn, g_ffn = _rec_inputs()

    def _L0_xattn_setup():
        import jax, jax.numpy as jnp
        import numpy as np
        D_MODEL = 128
        N_HEAD = 16
        D_H = D_MODEL // N_HEAD
        key = jax.random.key(seed)
        ks = jax.random.split(key, 12)
        B, LQ, LK = (4, 128, 256)
        s = 1.0 / np.sqrt(D_MODEL)
        inp = {'q_input': jax.random.normal(ks[0], (B, LQ, D_MODEL), jnp.float32), 'kv_input': jax.random.normal(ks[1], (B, LK, D_MODEL), jnp.float32), 'key_padding_mask': jax.random.randint(ks[2], (B, LK), 0, 2) > 0, 'W_Q': jax.random.normal(ks[3], (D_MODEL, D_MODEL), jnp.float32) * s, 'b_Q': jnp.zeros((D_MODEL,), jnp.float32), 'W_K': jax.random.normal(ks[4], (D_MODEL, D_MODEL), jnp.float32) * s, 'b_K': jnp.zeros((D_MODEL,), jnp.float32), 'W_V': jax.random.normal(ks[5], (D_MODEL, D_MODEL), jnp.float32) * s, 'b_V': jnp.zeros((D_MODEL,), jnp.float32), 'W_O': jax.random.normal(ks[6], (D_MODEL, D_MODEL), jnp.float32) * s, 'b_O': jnp.zeros((D_MODEL,), jnp.float32)}
        return inp
    _L0_xattn_all = _L0_xattn_setup()
    _L0_xattn_in = {k: v for k, v in _L0_xattn_all.items() if k in ('W_Q', 'b_Q', 'W_K', 'b_K', 'W_V', 'b_V', 'W_O', 'b_O')}
    del _L0_xattn_all

    def _L0_ffn_setup():
        import jax, jax.numpy as jnp
        import numpy as np
        B, S, D = (2, 128, 128)
        E, K, F, FS = (8, 2, 64, 128)
        key = jax.random.key(seed)
        ks = jax.random.split(key, 9)
        s = lambda k, shape, fan: jax.random.normal(k, shape, jnp.float32) * fan ** (-0.5)
        return {'x': jax.random.normal(ks[0], (B, S, D), jnp.float32), 'Wr': s(ks[1], (D, E), D), 'Wg': s(ks[2], (E, D, F), D), 'Wu': s(ks[3], (E, D, F), D), 'Wd': s(ks[4], (E, F, D), F), 'Sg': s(ks[5], (D, FS), D), 'Su': s(ks[6], (D, FS), D), 'Sd': s(ks[7], (FS, D), FS), 'expert_bias': jnp.zeros((E,), jnp.float32)}
    _L0_ffn_all = _L0_ffn_setup()
    _L0_ffn_in = {k: v for k, v in _L0_ffn_all.items() if k in ('Wr', 'Wg', 'Wu', 'Wd', 'Sg', 'Su', 'Sd', 'expert_bias')}
    del _L0_ffn_all
    return {'x': x, 'ctx_1024': ctx_1024, 'mask_BxS2_bk0': mask_BxS2_bk0, 'g_xattn': g_xattn, 'g_ffn': g_ffn, 'L0_xattn_W_Q': _L0_xattn_in['W_Q'], 'L0_xattn_b_Q': _L0_xattn_in['b_Q'], 'L0_xattn_W_K': _L0_xattn_in['W_K'], 'L0_xattn_b_K': _L0_xattn_in['b_K'], 'L0_xattn_W_V': _L0_xattn_in['W_V'], 'L0_xattn_b_V': _L0_xattn_in['b_V'], 'L0_xattn_W_O': _L0_xattn_in['W_O'], 'L0_xattn_b_O': _L0_xattn_in['b_O'], 'L0_ffn_Wr': _L0_ffn_in['Wr'], 'L0_ffn_Wg': _L0_ffn_in['Wg'], 'L0_ffn_Wu': _L0_ffn_in['Wu'], 'L0_ffn_Wd': _L0_ffn_in['Wd'], 'L0_ffn_Sg': _L0_ffn_in['Sg'], 'L0_ffn_Su': _L0_ffn_in['Su'], 'L0_ffn_Sd': _L0_ffn_in['Sd'], 'L0_ffn_expert_bias': _L0_ffn_in['expert_bias']}

def reference(x, ctx_1024, mask_BxS2_bk0, g_xattn, g_ffn, L0_xattn_W_Q, L0_xattn_b_Q, L0_xattn_W_K, L0_xattn_b_K, L0_xattn_W_V, L0_xattn_b_V, L0_xattn_W_O, L0_xattn_b_O, L0_ffn_Wr, L0_ffn_Wg, L0_ffn_Wu, L0_ffn_Wd, L0_ffn_Sg, L0_ffn_Su, L0_ffn_Sd, L0_ffn_expert_bias):
    import jax
    import jax.numpy as jnp

    def _L0_xattn_ref(q_input, kv_input, key_padding_mask, W_Q, b_Q, W_K, b_K, W_V, b_V, W_O, b_O):
        import jax, jax.numpy as jnp
        import numpy as np
        D_MODEL = 128
        N_HEAD = 16
        D_H = D_MODEL // N_HEAD
        B, LQ, _ = q_input.shape
        LK = kv_input.shape[1]
        q = q_input @ W_Q + b_Q
        k = kv_input @ W_K + b_K
        v = kv_input @ W_V + b_V
        q = q.reshape(B, LQ, N_HEAD, D_H).transpose(0, 2, 1, 3)
        k = k.reshape(B, LK, N_HEAD, D_H).transpose(0, 2, 1, 3)
        v = v.reshape(B, LK, N_HEAD, D_H).transpose(0, 2, 1, 3)
        sim = jnp.einsum('bhqd,bhkd->bhqk', q, k) / jnp.sqrt(jnp.float32(D_H))
        neg_inf = jnp.finfo(sim.dtype).min
        mask = key_padding_mask[:, None, None, :]
        sim = jnp.where(mask, neg_inf, sim)
        attn = jax.nn.softmax(sim, axis=-1)
        out = jnp.einsum('bhqk,bhkd->bhqd', attn, v)
        out = out.transpose(0, 2, 1, 3).reshape(B, LQ, D_MODEL)
        return out @ W_O + b_O

    def _L0_ffn_ref(x, Wr, Wg, Wu, Wd, Sg, Su, Sd, expert_bias):
        import jax, jax.numpy as jnp
        import numpy as np
        B, S, D = (2, 128, 128)
        E, K, F, FS = (8, 2, 64, 128)
        b, s, d = x.shape
        xf = x.reshape(-1, d)
        T = xf.shape[0]
        logits = xf @ Wr + expert_bias
        top_v, top_i = jax.lax.top_k(logits, K)
        probs = jax.nn.softmax(top_v, axis=-1)
        rw = jnp.zeros_like(logits).at[jnp.arange(T)[:, None], top_i].set(probs)
        gate = jnp.einsum('td,edf->tef', xf, Wg)
        up = jnp.einsum('td,edf->tef', xf, Wu)
        h = jax.nn.silu(gate) * up
        eo = jnp.einsum('tef,efd->ted', h, Wd)
        out = jnp.einsum('te,ted->td', rw, eo)
        out = out + jax.nn.silu(xf @ Sg) * (xf @ Su) @ Sd
        return out.reshape(b, s, d)
    x = x + jnp.tanh(g_xattn[0]) * _L0_xattn_ref(_layernorm(x, axis=-1), ctx_1024, mask_BxS2_bk0, L0_xattn_W_Q, L0_xattn_b_Q, L0_xattn_W_K, L0_xattn_b_K, L0_xattn_W_V, L0_xattn_b_V, L0_xattn_W_O, L0_xattn_b_O)
    x = x + jnp.tanh(g_ffn[0]) * _L0_ffn_ref(_layernorm(x, axis=-1), L0_ffn_Wr, L0_ffn_Wg, L0_ffn_Wu, L0_ffn_Wd, L0_ffn_Sg, L0_ffn_Su, L0_ffn_Sd, L0_ffn_expert_bias)
    return x

_drawn_inputs = setup_inputs


def setup_inputs(seed=0):
    import zlib

    import numpy as np

    out = dict(_drawn_inputs(seed))
    spreads = {'L0_xattn_b_Q': (0.0, 0.1),
     'L0_xattn_b_K': (0.0, 0.1),
     'L0_xattn_b_V': (0.0, 0.1),
     'L0_xattn_b_O': (0.0, 0.1),
     'L0_ffn_expert_bias': (0.0, 0.1)}
    factors = {}
    for name, (base, spread) in spreads.items():
        noise = np.random.default_rng([zlib.crc32(name.encode()), seed]).standard_normal(out[name].shape)
        drawn = base * np.exp(spread * noise) if base else spread * noise
        out[name] = jnp.asarray(drawn.astype(out[name].dtype))
    for name, factor in factors.items():
        out[name] = (out[name] * factor).astype(out[name].dtype)
    return out
```

```python
from contextlib import ExitStack

import concourse.bass as bass
from concourse import mybir

F32 = mybir.dt.float32
F32R = mybir.dt.float32r
U8 = mybir.dt.uint8
ALU = mybir.AluOpType
ACT = mybir.ActivationFunctionType
AX = mybir.AxisListType

P = 128
B = 4
S = 512
D = 128
NT = S // P
H = 16
DH = D // H
LK = 77
G = 4
HG = H // G
GR = HG * DH
TERMS = 3
KR = TERMS * GR
MR = 2 * HG
GK = HG * LK
HALF = 2 * GK
NC = 5
CH = 2 * NC
GS = 436
E = 8
FE = 64
EC = E * FE // P
FC = EC + 1
EPS = 1e-5
QB = 3
PR = 4
HR = 4
LAG = 2
LAST_ROUTE = 10
MAX_STEPS = [2, 2, 2, 2, 1, 1, 2]
MAXJ = [(0, 6), (6, 12), (12, 16)]


def chunk_rows(c):
    return min(P, HALF - P * c)


def kx_parts(half, c):
    parts = []
    if P * c < GK:
        parts.append((2 * half, 2 * half * GS + P * c))
    if P * c + chunk_rows(c) > GK:
        parts.append((2 * half + 1, 2 * half * GS + P + P * c))
    return parts


def drain_order():
    def keys(b):
        return [("k", b), ("v", b)] + [("vr", b, i) for i in range(3)]

    def maxima(b):
        return [("mx", b, i) for i in range(3 * NT)] + [("mt", b)]

    order = [("ct", b) for b in range(B)] + keys(0) + keys(1) + maxima(0)
    for b in range(B):
        if b + 1 < B:
            order += maxima(b + 1)
        if b + 2 < B:
            order += keys(b + 2)
    ups = [("up", n) for n in range(FC * B)]
    return order + ups[:LAST_ROUTE] + [("rt",)] + ups[LAST_ROUTE:]


def max_steps(i):
    return range(sum(MAX_STEPS[:i]), sum(MAX_STEPS[:i + 1]))


DRAIN = {use: n for n, use in enumerate(drain_order())}
CHUNK_ORDER = [FC - 1] + list(range(EC))


def build(nc, x, ctx, mask, g_att, g_ffn, w_q, b_q, w_k, b_k, w_v, b_v, w_o, b_o,
          w_r, w_g, w_u, w_d, s_g, s_u, s_d, e_bias, out):
    with ExitStack() as stack:
        def sb(name, shape, dt=F32):
            return stack.enter_context(nc.sbuf_tensor(name, shape, dt))

        def ps(name):
            return stack.enter_context(nc.psum_tensor(name, [P, 512], F32))

        def sem(name):
            return stack.enter_context(nc.semaphore(name))

        X = sb("X", [P, B, NT, D])
        XR = sb("XR", [P, B, NT, D])
        CTX = sb("CTX", [LK, B, D])
        MASK8 = sb("MASK8", [LK, B, LK], U8)
        WQ = sb("WQ", [D, D]); WK = sb("WK", [D, D]); WV = sb("WV", [D, D]); WO = sb("WO", [D, D])
        BQ = sb("BQ", [D, 1]); BV = sb("BV", [D, 1]); BO = sb("BO", [P, D])
        BK = sb("BK", [KR, G])
        GATES = sb("GATES", [P, 2]); TG = sb("TG", [P, 2])
        WR = sb("WR", [D, E]); EB = sb("EB", [P, E])
        WGU = sb("WGU", [D, 2, FC * P])
        WD = sb("WD", [P, FC, D])
        ID = sb("ID", [P, P])
        NEG_HALF = sb("NEG_HALF", [P, NT]); EULER = sb("EULER", [P, NT])
        RANK = sb("RANK", [P, E])
        WKX = sb("WKX", [D, G, TERMS, GR])
        WOG = sb("WOG", [D, D])
        BVB = sb("BVB", [D, P])
        BIAS = sb("BIAS", [P, D])
        SEL = sb("SEL", [LK, 3, LK], F32R)
        BD = sb("BD", [P, NC, H // 2, DH])
        MK = sb("MK", [KR, HG])
        MI = sb("MI", [P, HG])
        SELE0 = sb("SELE0", [2 * E, E])
        SELE = sb("SELE", [2 * E, E, FE], F32R)
        WGUH = sb("WGUH", [D, 2, FC * P], F32R); WGUL = sb("WGUL", [D, 2, FC * P], F32R)
        WRX = sb("WRX", [D, 2, E], F32R)
        WDG = sb("WDG", [P, FC, D])
        INV = sb("INV", [LK, B, LK]); VAL = sb("VAL", [LK, B, LK])
        MW = sb("MW", [LK, B, LK]); MW2 = sb("MW2", [LK, B, LK])
        NV = sb("NV", [LK, B]); NV1 = sb("NV1", [LK, B]); RNV = sb("RNV", [LK, B])
        VC = sb("VC", [LK, B]); ALLM = sb("ALLM", [LK, B]); VE = sb("VE", [LK, B])
        AI = sb("AI", [LK, B, 2, LK])
        CT = sb("CT", [D, B, 2, LK])
        ST1 = sb("ST1", [P, B, NT, 6]); MV1 = sb("MV1", [P, B, NT, 2])
        VE1 = sb("VE1", [P, B, NT]); RS1 = sb("RS1", [P, B, NT])
        XN = sb("XN", [P, 2, NT, D]); XNT = sb("XNT", [D, 2, S])
        QH = sb("QH", [D, 2, S], F32R); QL = sb("QL", [D, 2, S], F32R)
        QX = sb("QX", [KR + MR, QB, G, S], F32R)
        KF = sb("KF", [KR, 2, G, LK]); KS = sb("KS", [KR, 2, G, LK], F32R)
        KX = sb("KX", [KR + MR, QB, G * GS], F32R)
        VF = sb("VF", [LK, 2, 2, D // 2])
        VRH = sb("VRH", [LK, 2, 4, D // 2], F32R); VRL = sb("VRL", [LK, 2, 2, D // 2], F32R)
        VBD = sb("VBD", [P, QB, NC, 2, P])
        MX = sb("MX", [P, B, NT, H])
        MHL = sb("MHL", [P, B, NT, G, 2, HG], F32R)
        MT = sb("MT", [2 * H, 2, S], F32R)
        PROB = sb("PROB", [P, PR, S])
        LD = sb("LD", [P, S]); RD = sb("RD", [P, S])
        AT = sb("AT", [D, S])
        ST2 = sb("ST2", [P, B, NT, 6]); MV2 = sb("MV2", [P, B, NT, 2])
        VE2 = sb("VE2", [P, B, NT]); RS2 = sb("RS2", [P, B, NT])
        XN2 = sb("XN2", [P, NT, D])
        X2H = sb("X2H", [D, B, S], F32R); X2L = sb("X2L", [D, B, S], F32R)
        LG = sb("LG", [P, B, NT, E]); LG2 = sb("LG2", [P, B, NT, E])
        EQ = sb("EQ", [P, B, 2, NT, E]); CA = sb("CA", [P, B, 2, NT, E]); OH = sb("OH", [P, B, 2, NT, E])
        M12 = sb("M12", [P, B, 2, NT]); RK = sb("RK", [P, B, 2, NT])
        DM = sb("DM", [P, B, NT]); EX = sb("EX", [P, B, NT]); SM = sb("SM", [P, B, NT])
        W1 = sb("W1", [P, B, NT]); W2 = sb("W2", [P, B, NT])
        RA = sb("RA", [P, B, NT, E]); RB = sb("RB", [P, B, NT, E]); RW = sb("RW", [P, B, NT, E])
        RHL = sb("RHL", [P, B, NT, 2, E], F32R)
        RWT = sb("RWT", [2 * E, B, S], F32R)
        AR = sb("AR", [P, 2, S])
        SL, HID, OUT = XNT, PROB, XN

        dring = [ps("dring0"), ps("dring1")]
        sring = [ps("sring0"), ps("sring1")]
        acc = [ps("acc0"), ps("acc1")]
        pre = ps("pre")
        post = ps("post")

        d_x = [sem(f"d_x{b}") for b in range(B)]
        d_ctx = sem("d_ctx"); d_att = sem("d_att"); d_ffn = sem("d_ffn")
        d_wq = sem("d_wq"); d_wk = sem("d_wk"); d_wv = sem("d_wv"); d_gate = sem("d_gate"); d_ql = [sem(f"d_ql{b}") for b in range(B)]
        d_q = [sem(f"d_q{b}") for b in range(B)]
        d_m = [sem(f"d_m{b}") for b in range(B)]
        d_out = [sem(f"d_out{b}") for b in range(B)]
        pool_step = sem("pool_step")
        const_ready = sem("const_ready")
        xb_ready = sem("xb_ready"); rs1_ready = sem("rs1_ready"); rs2_ready = sem("rs2_ready")
        ex_ready = sem("ex_ready"); wffn_ready = sem("wffn_ready")
        dve = sem("dve")
        prep = sem("prep")
        var1_ready = sem("var1_ready"); xn_ready = sem("xn_ready"); ql_ready = sem("ql_ready")
        ct_ready = sem("ct_ready"); ks_ready = sem("ks_ready"); vr_ready = sem("vr_ready")
        vbd_ready = sem("vbd_ready"); mhl_ready = sem("mhl_ready");
        bias_ready = sem("bias_ready")
        drained = sem("drained")
        at_ready = sem("at_ready"); x1_ready = sem("x1_ready"); var2_ready = sem("var2_ready")
        xn2_ready = sem("xn2_ready"); x2l_ready = sem("x2l_ready"); lg_ready = sem("lg_ready")
        dm_ready = sem("dm_ready"); rhl_ready = sem("rhl_ready")
        ar_ready = sem("ar_ready"); out_ready = sem("out_ready")
        tanh_ready = sem("tanh_ready"); ind_ready = sem("ind_ready")
        xnt_ready = sem("xnt_ready"); qh_ready = sem("qh_ready"); kx_ready = sem("kx_ready")
        exp_ready = sem("exp_ready"); ln_ready = sem("ln_ready"); rd_ready = sem("rd_ready")
        x2h_ready = sem("x2h_ready"); rwt_ready = sem("rwt_ready"); silu_ready = sem("silu_ready")
        filled = sem("filled")
        t1_done = sem("t1_done"); q_done = sem("q_done"); bo_done = sem("bo_done")
        s_done = sem("s_done"); pv_done = sem("pv_done");
        o_done = sem("o_done"); t2_done = sem("t2_done"); lg_done = sem("lg_done"); rt_done = sem("rt_done")
        gate_done = sem("gate_done"); rw_done = sem("rw_done"); y_chunk = sem("y_chunk"); y_done = sem("y_done")

        PREP_WK, PREP_SEL, PREP_MK, PREP_MI, PREP_WO, PREP_BVB, PREP_SELE = range(1, 8)
        CONST_ID, CONST_PAD, CONST_POW, CONST_BD, CONST_RANK = 1, 2, 3, 4, 5

        block = stack.enter_context(nc.Block())

        def tok(ap, b):
            return ap.rearrange("b (p t) d -> b p t d", t=NT)[b]

        def col(ap):
            return ap.rearrange("(p o) -> p o", o=1)

        def on_all(ap, n):
            return ap.rearrange("(o k) -> o k", o=1).to_broadcast([n, ap.shape[0]])

        @block.sync
        def _(sp):
            sp.dma_start(X[:, 0], tok(x, 0)).then_inc(d_x[0], 16)
            sp.dma_start(MASK8[:], mask.rearrange("(o b) k -> o b k", o=1).to_broadcast([LK, B, LK])).then_inc(d_ctx, 16)
            sp.dma_start(CTX[:], ctx.rearrange("b k d -> k b d")).then_inc(d_ctx, 16)
            sp.dma_start(X[:, 1], tok(x, 1)).then_inc(d_x[1], 16)
            sp.dma_start(WV[:], w_v).then_inc(d_wv, 16)

            def send_q(b):
                if b >= QB:
                    sp.wait_ge(s_done, CH * (b - QB + 1))
                sp.wait_ge(qh_ready, b + 1)
                sp.wait_ge(ql_ready, b + 1)
                for g in range(G):
                    rows = slice(GR * g, GR * g + GR)
                    for term, src in enumerate((QH, QH, QL)):
                        sp.dma_start(QX[GR * term:GR * term + GR, b % QB, g, :].bitcast(F32),
                                     src[rows, b % 2, :].bitcast(F32)).then_inc(d_q[b], 16)

            def send_max(b):
                if b >= QB:
                    sp.wait_ge(s_done, CH * (b - QB + 1))
                sp.wait_ge(drained, DRAIN[("mt", b)] + 1)
                for g in range(G):
                    sp.dma_start(QX[KR:KR + MR, b % QB, g, :].bitcast(F32),
                                 MT[MR * g:MR * g + MR, b % 2, :].bitcast(F32)).then_inc(d_m[b], 16)

            send_q(0)
            sp.dma_start(X[:, 2], tok(x, 2)).then_inc(d_x[2], 16)
            send_q(1)
            sp.dma_start(X[:, 3], tok(x, 3)).then_inc(d_x[3], 16)
            send_max(0)
            sp.dma_start(WGU[:, 0, 0:EC * P].rearrange("d (e f) -> d e f", e=E), w_g.rearrange("e d f -> d e f")).then_inc(d_ffn, 16)
            sp.dma_start(WGU[:, 1, 0:EC * P].rearrange("d (e f) -> d e f", e=E), w_u.rearrange("e d f -> d e f")).then_inc(d_ffn, 16)
            sp.dma_start(WGU[:, 0, EC * P:], s_g).then_inc(d_ffn, 16)
            sp.dma_start(WGU[:, 1, EC * P:], s_u).then_inc(d_ffn, 16)
            sp.dma_start(WD[:, 0:EC, :], w_d.rearrange("(c e) f d -> (e f) c d", c=EC)).then_inc(d_ffn, 16)
            sp.dma_start(WD[:, EC, :], s_d).then_inc(d_ffn, 16)
            sp.dma_start(WR[:], w_r).then_inc(d_ffn, 16)
            for b in range(B):
                if b + 2 < B:
                    send_q(b + 2)
                if b + 1 < B:
                    send_max(b + 1)
            for b in range(B):
                sp.wait_ge(out_ready, b + 1)
                sp.dma_start(tok(out, b), OUT[:, b % 2]).then_inc(d_out[b], 16)
            for b in range(B):
                sp.wait_ge(d_out[b], 16)

        @block.gpsimd
        def _(pool):
            steps = [0]

            def step(ins):
                steps[0] += 1
                ins.then_inc(pool_step, 1)
                pool.wait_ge(pool_step, steps[0])

            step(pool.memset(ID[:], 0.0))
            pool.affine_select(out=ID[:], in_=ID[:], compare_op=ALU.not_equal, fill=1.0, base=0,
                               pattern=[[-1, P]], channel_multiplier=1).then_inc(const_ready, 1)
            step(pool.memset(NEG_HALF[:], -0.5))
            step(pool.memset(EULER[:], 2.718281828459045))
            pad = KX[:].rearrange("p s (g c) -> p (s g) c", g=G)[:, :, GK:GS]
            pool.memset(pad.bitcast(F32), 0.0).then_inc(const_ready, 1)

            def rstd(mv, ve, rs, b, ready):
                step(pool.tensor_scalar(ve[:, b], mv[:, b, :, 1], EPS, None, ALU.add))
                pool.tensor_tensor(rs[:, b], ve[:, b], NEG_HALF[:], ALU.pow).then_inc(ready, 1)

            pool.wait_ge(var1_ready, 1)
            rstd(MV1, VE1, RS1, 0, rs1_ready)
            pool.dma_start(WO[:], w_o).then_inc(d_att, 16)
            pool.dma_start(BV[:], col(b_v)).then_inc(d_att, 16)
            pool.dma_start(BO[:], on_all(b_o, P)).then_inc(d_att, 16)
            pool.dma_start(EB[:], on_all(e_bias, P)).then_inc(d_att, 16)
            step(pool.memset(BD[:], 1.0))
            step(pool.affine_select(out=BD[:], in_=BD[:], compare_op=ALU.is_ge, fill=0.0, base=0,
                                    pattern=[[P, NC], [-LK, H // 2], [0, DH]], channel_multiplier=1))
            pool.affine_select(out=BD[:], in_=BD[:], compare_op=ALU.is_ge, fill=0.0, base=LK - 1,
                               pattern=[[-P, NC], [LK, H // 2], [0, DH]], channel_multiplier=-1).then_inc(const_ready, 2)
            pool.wait_ge(var1_ready, 2)
            rstd(MV1, VE1, RS1, 1, rs1_ready)
            for e in range(E):
                last = pool.memset(RANK[:, e:e + 1], float(E - e))
                if e < E - 1:
                    step(last)
            last.then_inc(const_ready, 1)

            def residual_bias(b):
                pool.wait_ge(d_x[b], 16)
                pool.wait_ge(bias_ready, 1)
                pool.tensor_tensor(XR[:, b], X[:, b], BIAS[:].unsqueeze(1).to_broadcast([P, NT, D]), ALU.add).then_inc(xb_ready, 1)

            residual_bias(0)
            pool.wait_ge(var1_ready, 3)
            rstd(MV1, VE1, RS1, 2, rs1_ready)
            pool.wait_ge(d_ffn, 16 * 7)
            pool.tensor_copy(WGUH[:], WGU[:]).then_inc(wffn_ready, 1)
            pool.tensor_copy(WRX[:, 0], WR[:]).then_inc(wffn_ready, 1)
            pool.wait_ge(wffn_ready, 2)
            pool.tensor_tensor(WRX[:, 1], WR[:], WRX[:, 0].bitcast(F32), ALU.subtract).then_inc(wffn_ready, 1)
            pool.wait_ge(var1_ready, 4)
            rstd(MV1, VE1, RS1, 3, rs1_ready)
            pool.tensor_tensor(WGUL[:], WGU[:], WGUH[:].bitcast(F32), ALU.subtract).then_inc(wffn_ready, 1)
            pool.wait_ge(tanh_ready, 1)
            pool.tensor_scalar(WDG[:], WD[:], TG[:, 1:2], None, ALU.mult).then_inc(wffn_ready, 1)
            for b in range(B):
                if b + 1 < B:
                    residual_bias(b + 1)
                pool.wait_ge(var2_ready, b + 1)
                rstd(MV2, VE2, RS2, b, rs2_ready)
                pool.wait_ge(dm_ready, b + 1)
                pool.tensor_tensor(EX[:, b], EULER[:], DM[:, b], ALU.pow).then_inc(ex_ready, 1)

        @block.scalar
        def _(act):
            act.dma_start(GATES[:, 0:1], on_all(g_att, P)).then_inc(d_gate, 16)
            act.dma_start(GATES[:, 1:2], on_all(g_ffn, P)).then_inc(d_gate, 16)
            act.dma_start(WQ[:], w_q).then_inc(d_wq, 16)
            act.dma_start(BQ[:], col(b_q)).then_inc(d_wq, 16)
            act.dma_start(WK[:], w_k).then_inc(d_wk, 16)
            for term in range(TERMS):
                act.dma_start(BK[GR * term:GR * term + GR, :], b_k).then_inc(d_wk, 16)
            act.wait_ge(d_gate, 32)
            act.activation(TG[:], GATES[:], ACT.Tanh).then_inc(tanh_ready, 1)
            nc.scalar.preload_act_table_set("natural_log_exp_and_others")

            def xnt(b):
                act.wait_ge(t1_done, b + 1)
                if b >= 2:
                    act.wait_ge(q_done, b - 1)
                act.activation(XNT[:, b % 2], pre[:], ACT.Copy).then_inc(xnt_ready, 1)

            def qh(b):
                act.wait_ge(q_done, b + 1)
                if b >= 2:
                    act.wait_ge(d_q[b - 2], 16 * TERMS * G)
                act.activation(QH[:, b % 2], pre[:], ACT.Identity, bias=BQ[:]).then_inc(qh_ready, 1)

            def indicator(s):
                act.activation(KX[KR:KR + MR, s].rearrange("p (g c) -> p g c", g=G)[:, :, 0:GK]
                               .rearrange("p g (h k) -> p g h k", h=HG),
                               MI[KR:KR + MR, :].unsqueeze(1).unsqueeze(3).to_broadcast([MR, G, HG, LK]),
                               ACT.Copy).then_inc(ind_ready, 1)

            def kx(b):
                act.wait_ge(ks_ready, b + 1)
                if b >= QB:
                    act.wait_ge(s_done, CH * (b - QB + 1))
                for h in range(HG):
                    act.activation(KX[0:KR, b % QB].rearrange("p (g c) -> p g c", g=G)[:, :, LK * h:LK * h + LK],
                                   KS[:, b % 2].bitcast(F32), ACT.Copy, scale=MK[:, h:h + 1]).then_inc(kx_ready, 1)

            def exp(b, i):
                n = CH * b + i
                rows = chunk_rows(i % NC)
                act.wait_ge(s_done, n + 1)
                if n >= PR:
                    act.wait_ge(pv_done, n - PR + 1)
                act.activation(PROB[0:rows, n % PR], sring[n % 2][0:rows, :], ACT.Exp, scale=DH ** -0.5).then_inc(exp_ready, 1)

            def inverse(b, half):
                n = 2 * b + half
                num, den = (slice(0, 64), slice(64, P)) if half == 0 else (slice(64, P), slice(0, 64))
                act.wait_ge(pv_done, NC * (n + 1))
                act.activation(LD[num], acc[n % 2][den, :], ACT.Ln).then_inc(ln_ready, 1)
                act.wait_ge(ln_ready, n + 1)
                if n >= 2:
                    act.wait_ge(at_ready, n - 1)
                act.activation(RD[num], LD[num], ACT.Exp, scale=-1.0).then_inc(rd_ready, 1)

            def x2h(b):
                act.wait_ge(t2_done, b + 1)
                act.activation(X2H[:, b], post[:], ACT.Copy).then_inc(x2h_ready, 1)

            def rwt(b):
                act.wait_ge(rt_done, b + 1)
                act.activation(RWT[:, b], post[0:2 * E, :], ACT.Copy).then_inc(rwt_ready, 1)

            xnt(0)
            qh(0)
            act.wait_ge(prep, PREP_MI)
            indicator(0)
            xnt(1)
            qh(1)
            kx(0)
            indicator(1)
            kx(1)
            indicator(2)
            for b in range(B):
                for i in range(CH + LAG):
                    if i < CH:
                        exp(b, i)
                    if i == 0 and b >= 1:
                        inverse(b - 1, 1)
                    if i == 0 and b + 2 < B:
                        xnt(b + 2)
                    if i == 1 and b + 2 < B:
                        qh(b + 2)
                    if i == NC + LAG:
                        inverse(b, 0)
                    if i == 7 and b >= 1:
                        x2h(b - 1)
                    if i == 9 and b + 2 < B:
                        kx(b + 2)
                    if i == 11 and b >= 1:
                        rwt(b - 1)
            inverse(B - 1, 1)
            for n in range(FC * B):
                act.wait_ge(gate_done, n + 1)
                if n >= 2:
                    act.wait_ge(drained, DRAIN[("up", n - 2)] + 1)
                act.activation(SL[:, n % 2], sring[n % 2][:], ACT.Silu).then_inc(silu_ready, 1)
                if n == 3:
                    x2h(B - 1)

        @block.vector
        def _(v):
            steps = [0]

            def step(ins):
                steps[0] += 1
                ins.then_inc(dve, 1)
                v.wait_ge(dve, steps[0])

            def mark(ins):
                steps[0] += 1
                ins.then_inc(dve, 1)
                return steps[0]

            def stats(src, st, mv, b, ready):
                for t in range(NT):
                    m = mark(v.bn_stats(st[:, b, t], src[:, b, t]))
                v.wait_ge(dve, m)
                for t in range(NT):
                    last = v.bn_aggr(mv[:, b, t], st[:, b, t])
                    if t < NT - 1:
                        mark(last)
                last.then_inc(ready, 1)

            def ln1_stats(b):
                v.wait_ge(d_x[b], 16)
                stats(X, ST1, MV1, b, var1_ready)

            def ln1_apply(b):
                v.wait_ge(rs1_ready, b + 1)
                if b >= 2:
                    v.wait_ge(t1_done, b - 1)
                for t in range(NT):
                    v.tensor_scalar(XN[:, b % 2, t], X[:, b, t], MV1[:, b, t, 0:1], RS1[:, b, t:t + 1],
                                    ALU.subtract, ALU.mult).then_inc(xn_ready, 1)

            def ql(b):
                v.wait_ge(q_done, b + 1)
                v.wait_ge(qh_ready, b + 1)
                if b >= 2:
                    v.wait_ge(d_q[b - 2], 16 * TERMS * G)
                v.scalar_tensor_tensor(QL[:, b % 2], pre[:], BQ[:], QH[:, b % 2].bitcast(F32), ALU.add, ALU.subtract).then_inc(ql_ready, 1)

            def full(use):
                v.wait_ge(filled, DRAIN[use] + 1)
                return dring[DRAIN[use] % 2]

            def keys_k(b):
                bank = full(("k", b))
                v.tensor_tensor(KF[:, b % 2], bank[0:KR, 0:GK].rearrange("p (g k) -> p g k", g=G),
                                BK[:].unsqueeze(2).to_broadcast([KR, G, LK]), ALU.add).then_inc(drained, 1)
                v.wait_ge(drained, DRAIN[("k", b)] + 1)
                if b >= 2:
                    v.wait_ge(kx_ready, HG * (b - 1))
                step(v.tensor_copy(KS[:, b % 2], KF[:, b % 2]))
                lo = slice(GR, 2 * GR)
                v.tensor_tensor(KS[lo, b % 2], KF[lo, b % 2], KS[lo, b % 2].bitcast(F32), ALU.subtract).then_inc(ks_ready, 1)

            def keys_v(b):
                bank = full(("v", b))
                v.tensor_scalar(VF[:, b % 2], bank[0:LK, 0:D].rearrange("p (a c) -> p a c", a=2), VE[:, b:b + 1], None, ALU.mult).then_inc(drained, 1)
                v.wait_ge(drained, DRAIN[("v", b)] + 1)
                if b >= 2:
                    v.wait_ge(filled, DRAIN[("vr", b - 2, 2)] + 1)
                mark(v.tensor_copy(VRH[:, b % 2, 0:4:3], VF[:, b % 2]))
                step(v.tensor_copy(VRH[:, b % 2, 1:3], VE[:, b:b + 1].unsqueeze(2).to_broadcast([LK, 2, D // 2])))
                v.tensor_tensor(VRL[:, b % 2], VF[:, b % 2], VRH[:, b % 2, 0:4:3].bitcast(F32), ALU.subtract).then_inc(vr_ready, 1)

            def keys_vr(b, i):
                bank = full(("vr", b, i))
                first, last = 2 * i, min(2 * i + 2, NC)
                if i == 0 and b >= QB:
                    v.wait_ge(pv_done, CH * (b - QB + 1))
                v.tensor_tensor(VBD[:, b % QB, first:last].rearrange("p c a (t n) -> p c (a t) n", t=2),
                                bank[:, 0:(last - first) * 2 * P].rearrange("p (c q n) -> p c q n", q=4, n=P // 2),
                                BD[:, first:last].rearrange("p c h d -> p c (h d)").unsqueeze(2).to_broadcast([P, last - first, 4, P // 2]),
                                ALU.mult).then_inc(drained, 1)

            def maximum(b, n):
                bank = full(("mx", b, n))
                h0, h1 = MAXJ[n % 3]
                v.tensor_reduce(MX[:, b, n // 3, h0:h1], bank[:, 0:(h1 - h0) * LK].rearrange("p (h k) -> p h k", k=LK), AX.X, ALU.max).then_inc(drained, 1)

            def split_max(b):
                v.wait_ge(drained, DRAIN[("mx", b, 3 * NT - 1)] + 1)
                mx = MX[:, b].rearrange("p t (g r) -> p (t g) r", g=G)
                hl = MHL[:, b].rearrange("p t g m r -> p (t g) m r")
                step(v.tensor_scalar(hl[:, :, 0, :], mx, -1.0, None, ALU.mult))
                v.scalar_tensor_tensor(hl[:, :, 1, :], mx, -1.0, hl[:, :, 0, :].bitcast(F32), ALU.mult, ALU.subtract).then_inc(mhl_ready, 1)

            def max_rows(b):
                bank = full(("mt", b))
                if b >= 2:
                    v.wait_ge(d_m[b - 2], 16 * G)
                v.tensor_copy(MT[:, b % 2], bank[0:2 * H, :]).then_inc(drained, 1)

            def normalise(b, half):
                n = 2 * b + half
                num = slice(0, 64) if half == 0 else slice(64, P)
                v.wait_ge(rd_ready, n + 1)
                if b >= 1:
                    v.wait_ge(o_done, b)
                v.tensor_tensor(AT[num], acc[n % 2][num, :], RD[num], ALU.mult).then_inc(at_ready, 1)

            def residual(b):
                v.wait_ge(o_done, b + 1)
                v.wait_ge(xb_ready, b + 1)
                v.tensor_tensor(XR[:, b].rearrange("p t d -> p (t d)"), post[:], XR[:, b].rearrange("p t d -> p (t d)"), ALU.add).then_inc(x1_ready, 1)
                v.wait_ge(x1_ready, b + 1)
                stats(XR, ST2, MV2, b, var2_ready)

            def ln2_apply(b):
                v.wait_ge(rs2_ready, b + 1)
                if b >= 1:
                    v.wait_ge(t2_done, b)
                for t in range(NT):
                    v.tensor_scalar(XN2[:, t], XR[:, b, t], MV2[:, b, t, 0:1], RS2[:, b, t:t + 1],
                                    ALU.subtract, ALU.mult).then_inc(xn2_ready, 1)

            def x2l(b):
                v.wait_ge(x2h_ready, b + 1)
                v.tensor_tensor(X2L[:, b], post[:], X2H[:, b].bitcast(F32), ALU.subtract).then_inc(x2l_ready, 1)

            def over_experts(a):
                return a.unsqueeze(2).to_broadcast([P, NT, E])

            def over_tiles(a):
                return a.unsqueeze(1).to_broadcast([P, NT, E])

            def pick(b, k, logits):
                step(v.tensor_reduce(M12[:, b, k], logits, AX.X, ALU.max))
                step(v.tensor_tensor(EQ[:, b, k], logits, over_experts(M12[:, b, k]), ALU.is_equal))
                step(v.tensor_tensor(CA[:, b, k], EQ[:, b, k], over_tiles(RANK[:]), ALU.mult))
                step(v.tensor_reduce(RK[:, b, k], CA[:, b, k], AX.X, ALU.max))
                step(v.tensor_tensor(OH[:, b, k], over_tiles(RANK[:]), over_experts(RK[:, b, k]), ALU.is_equal))

            def route_pick(b):
                v.wait_ge(lg_done, b + 1)
                if b == 0:
                    v.wait_ge(const_ready, CONST_RANK)
                v.tensor_reduce(LG2[:, b], post[:, 0:NT * 2 * E].rearrange("p (t m e) -> p t e m", t=NT, m=2), AX.X, ALU.add).then_inc(lg_ready, 1)
                v.wait_ge(lg_ready, b + 1)
                step(v.tensor_tensor(LG[:, b], LG2[:, b], over_tiles(EB[:]), ALU.add))
                pick(b, 0, LG[:, b])
                step(v.scalar_tensor_tensor(LG2[:, b], OH[:, b, 0], -3.0e38, LG[:, b], ALU.mult, ALU.add))
                pick(b, 1, LG2[:, b])
                v.tensor_tensor(DM[:, b], M12[:, b, 1], M12[:, b, 0], ALU.subtract).then_inc(dm_ready, 1)

            def route_weights(b):
                v.wait_ge(ex_ready, b + 1)
                step(v.tensor_scalar(SM[:, b], EX[:, b], 1.0, None, ALU.add))
                step(v.reciprocal(W1[:, b], SM[:, b]))
                step(v.tensor_tensor(W2[:, b], EX[:, b], W1[:, b], ALU.mult))
                mark(v.tensor_tensor(RA[:, b], OH[:, b, 0], over_experts(W1[:, b]), ALU.mult))
                step(v.tensor_tensor(RB[:, b], OH[:, b, 1], over_experts(W2[:, b]), ALU.mult))
                step(v.tensor_tensor(RW[:, b], RA[:, b], RB[:, b], ALU.add))
                step(v.tensor_copy(RHL[:, b, :, 0], RW[:, b]))
                v.tensor_tensor(RHL[:, b, :, 1], RW[:, b], RHL[:, b, :, 0].bitcast(F32), ALU.subtract).then_inc(rhl_ready, 1)

            def finish_rows(b):
                v.wait_ge(y_done, b + 1)
                if b >= 2:
                    v.wait_ge(d_out[b - 2], 16)
                bank = (pre, post)[b % 2]
                v.tensor_tensor(OUT[:, b % 2].rearrange("p t d -> p (t d)"), bank[:], XR[:, b].rearrange("p t d -> p (t d)"), ALU.add).then_inc(out_ready, 1)

            ln1_stats(0)
            v.wait_ge(const_ready, CONST_ID)
            v.wait_ge(d_ctx, 32)
            step(v.tensor_copy(INV[:], MASK8[:]))
            mark(v.tensor_reduce(NV[:], INV[:], AX.X, ALU.add))
            ident = ID[0:LK, 0:LK].unsqueeze(1).to_broadcast([LK, B, LK])
            step(v.tensor_tensor(VAL[:], INV[:], ident, ALU.mult))
            ln1_apply(0)
            mark(v.tensor_reduce(VC[:], VAL[:], AX.X, ALU.add))
            step(v.tensor_scalar(NV1[:], NV[:], -1.0, float(LK), ALU.mult, ALU.add))
            step(v.tensor_scalar(ALLM[:], NV1[:], 0.0, None, ALU.is_equal))
            step(v.tensor_scalar(NV1[:], NV1[:], 1.0, None, ALU.max))
            step(v.reciprocal(RNV[:], NV1[:]))
            step(v.tensor_scalar(VC[:], VC[:], -1.0, 1.0, ALU.mult, ALU.add))
            mark(v.tensor_tensor(VE[:], VC[:], ALLM[:], ALU.add))
            step(v.tensor_tensor(MW[:], INV[:], RNV[:].unsqueeze(2).to_broadcast([LK, B, LK]), ALU.mult))
            step(v.tensor_tensor(MW2[:], MW[:], ident, ALU.add))
            mark(v.tensor_copy(AI[:, :, 1], ident))
            step(v.tensor_tensor(AI[:, :, 0], MW2[:], VC[:].unsqueeze(2).to_broadcast([LK, B, LK]), ALU.mult))
            v.wait_ge(d_wk, 64)
            v.tensor_copy(WKX[:], WK[:].rearrange("p (g r) -> p g r", g=G).unsqueeze(2).to_broadcast([D, G, TERMS, GR])).then_inc(prep, 1)
            v.tensor_copy(SEL[:], ID[0:LK, 0:LK].unsqueeze(1).to_broadcast([LK, 3, LK])).then_inc(prep, 1)
            v.tensor_reduce(MK[:], ID[0:KR, 0:KR].rearrange("p (j h d) -> p h j d", j=TERMS, h=HG), AX.XY, ALU.add).then_inc(prep, 1)
            v.tensor_reduce(MI[KR:KR + MR], ID[KR:KR + MR, KR:KR + MR].rearrange("p (j h) -> p h j", h=HG), AX.X, ALU.add).then_inc(prep, 1)
            ql(0)
            ln1_stats(1)
            for b in range(B):
                bank = full(("ct", b))
                v.tensor_copy(CT[:, b].rearrange("p a k -> p (a k)"), bank[:, 0:2 * LK]).then_inc(drained, 1)
            ln1_apply(1)
            keys_k(0)
            keys_v(0)
            v.wait_ge(const_ready, CONST_BD)
            for i in range(3):
                keys_vr(0, i)
            ql(1)
            keys_k(1)
            keys_v(1)
            for i in range(3):
                keys_vr(1, i)
            v.wait_ge(tanh_ready, 1)
            v.wait_ge(d_att, 64)
            v.tensor_scalar(WOG[:], WO[:], TG[:, 0:1], None, ALU.mult).then_inc(prep, 1)
            v.tensor_copy(BVB[:], BV[:].to_broadcast([D, P])).then_inc(prep, 1)
            v.tensor_reduce(SELE0[:], ID[0:2 * E, 0:2 * E].rearrange("p (j e) -> p e j", j=2), AX.X, ALU.add).then_inc(prep, 1)
            v.wait_ge(prep, PREP_SELE)
            mark_sele = mark(v.tensor_copy(SELE[:], SELE0[:].unsqueeze(2).to_broadcast([2 * E, E, FE])))
            for n in range(3 * NT):
                maximum(0, n)
            split_max(0)
            v.wait_ge(bo_done, 1)
            v.scalar_tensor_tensor(BIAS[:], BO[:], TG[:, 0:1], post[:, 0:D], ALU.mult, ALU.add).then_inc(bias_ready, 1)
            max_rows(0)
            ln1_stats(2)
            ln1_apply(2)
            for b in range(B):
                for i in range(CH + LAG):
                    if b + 1 < B:
                        for n in max_steps(i):
                            maximum(b + 1, n)
                    if i == 1 and b >= 1:
                        normalise(b - 1, 1)
                    if i == 2 and b + 2 < B:
                        ql(b + 2)
                    if i == 4 and b >= 1:
                        residual(b - 1)
                    if i == 6 and b + 1 < B:
                        split_max(b + 1)
                    if i == 5 and b >= 1:
                        ln2_apply(b - 1)
                    if i == 7 and b >= 1:
                        x2l(b - 1)
                    if i == 8 and b + 1 < B:
                        max_rows(b + 1)
                    if i == 8 and b + 2 < B:
                        keys_k(b + 2)
                    if i == 7 and b + 3 < B:
                        ln1_stats(b + 3)
                    if i == 8:
                        normalise(b, 0)
                    if i == 8 and b + 2 < B:
                        keys_v(b + 2)
                    if i == 9 and b + 3 < B:
                        ln1_apply(b + 3)
                    if i == 9 and b >= 1:
                        route_pick(b - 1)
                    if i >= 9 and b + 2 < B:
                        keys_vr(b + 2, i - 9)
                    if i == 10 and b >= 1:
                        route_weights(b - 1)
            normalise(B - 1, 1)
            for n in range(FC * B):
                c = CHUNK_ORDER[n % FC]
                b = n // FC
                bank = full(("up", n))
                if n >= HR:
                    v.wait_ge(y_chunk, n - HR + 1)
                v.wait_ge(silu_ready, n + 1)
                if c == FC - 1:
                    v.tensor_tensor(HID[:, n % HR], SL[:, n % 2], bank[:], ALU.mult).then_inc(drained, 1)
                else:
                    v.wait_ge(rw_done, EC * b + c + 1)
                    v.tensor_tensor(AR[:, n % 2], SL[:, n % 2], acc[c % 2][:], ALU.mult).then_inc(ar_ready, 1)
                    v.wait_ge(ar_ready, EC * b + c + 1)
                    v.tensor_tensor(HID[:, n % HR], AR[:, n % 2], bank[:], ALU.mult).then_inc(drained, 1)
                if n == 1:
                    residual(B - 1)
                if n == 2:
                    ln2_apply(B - 1)
                if n == 3:
                    x2l(B - 1)
                if n == 4:
                    route_pick(B - 1)
                if n == 6:
                    route_weights(B - 1)
                if n == LAST_ROUTE - 1:
                    v.tensor_copy(RWT[:, B - 1], full(("rt",))[0:2 * E, :]).then_inc(drained, 1)
                if n % FC == 2 and n > FC:
                    finish_rows(n // FC - 1)
            finish_rows(B - 1)

        @block.tensor
        def _(pe):
            def drained_bank(use):
                n = DRAIN[use]
                if n >= 2:
                    pe.wait_ge(drained, n - 1)
                return dring[n % 2]

            def t1(b):
                pe.wait_ge(xn_ready, NT * (b + 1))
                if b >= 1:
                    pe.wait_ge(qh_ready, b)
                    pe.wait_ge(ql_ready, b)
                for t in range(NT):
                    last = pe.transpose(pre[:, P * t:P * t + P], XN[:, b % 2, t], ID[:])
                last.then_inc(t1_done, 1)

            def q(b):
                pe.wait_ge(xnt_ready, b + 1)
                pe.matmul(pre[:], WQ[:], XNT[:, b % 2], start=True, stop=True).then_inc(q_done, 1)

            def context(b):
                bank = drained_bank(("ct", b))
                pe.matmul(bank[:, 0:2 * LK], CTX[:, b], AI[:, b].rearrange("p a k -> p (a k)"), start=True, stop=True).then_inc(filled, 1)

            def keys_k(b):
                bank = drained_bank(("k", b))
                pe.wait_ge(drained, DRAIN[("ct", b)] + 1)
                for g in range(G):
                    last = pe.matmul(bank[0:KR, LK * g:LK * g + LK], WKX[:, g].rearrange("p a r -> p (a r)"), CT[:, b, 0],
                                     start=True, stop=True)
                last.then_inc(filled, 1)

            def keys_v(b):
                bank = drained_bank(("v", b))
                pe.matmul(bank[0:LK, 0:D], CT[:, b, 1], WV[:], start=True, stop=True).then_inc(filled, 1)

            def keys_vr(b, i):
                bank = drained_bank(("vr", b, i))
                pe.wait_ge(vr_ready, b + 1)
                sel = SEL[:].rearrange("p a k -> p (a k)")
                for c in range(2 * i, min(2 * i + 2, NC)):
                    at = P * c % LK
                    both = bank[:, 2 * P * (c - 2 * i):2 * P * (c - 2 * i + 1)]
                    pe.matmul(both, sel[:, at:at + P], VRH[:, b % 2].rearrange("p a n -> p (a n)"), start=True, stop=False)
                    last = pe.matmul(both.rearrange("p (q n) -> p q n", q=4)[:, 0:4:3], sel[:, at:at + P], VRL[:, b % 2],
                                     start=False, stop=True)
                last.then_inc(filled, 1)

            def maximum(b, n):
                bank = drained_bank(("mx", b, n))
                t = n // 3
                h0, h1 = MAXJ[n % 3]
                h = h0
                while h < h1:
                    g, end = h // HG, min(h1, (h // HG + 1) * HG)
                    at = GS * g + LK * (h - HG * g)
                    last = pe.matmul(bank[:, LK * (h - h0):LK * (end - h0)], QX[0:KR, b % QB, g, P * t:P * t + P],
                                     KX[0:KR, b % QB, at:at + LK * (end - h)], start=True, stop=True)
                    h = end
                last.then_inc(filled, 1)

            def max_rows(b):
                bank = drained_bank(("mt", b))
                pe.wait_ge(mhl_ready, b + 1)
                for t in range(NT):
                    last = pe.transpose(bank[0:2 * H, P * t:P * t + P], MHL[:, b, t].rearrange("p g m r -> p (g m r)").bitcast(F32), ID[:])
                last.then_inc(filled, 1)

            def scores(b, i):
                n = CH * b + i
                half, c = i // NC, i % NC
                rows = chunk_rows(c)
                if n >= 2:
                    pe.wait_ge(exp_ready, n - 1)
                parts = kx_parts(half, c)
                for k, (g, at) in enumerate(parts):
                    last = pe.matmul(sring[n % 2][0:rows, :], KX[:, b % QB, at:at + rows], QX[:, b % QB, g],
                                     start=(k == 0), stop=(k == len(parts) - 1))
                last.then_inc(s_done, 1)

            def weigh(b, i):
                n = CH * b + i
                half, c = i // NC, i % NC
                rows = chunk_rows(c)
                if c == 0 and 2 * b + half >= 2:
                    pe.wait_ge(at_ready, 2 * b + half - 1)
                pe.wait_ge(exp_ready, n + 1)
                last = pe.matmul(acc[(2 * b + half) % 2][:], VBD[0:rows, b % QB, c, half], PROB[0:rows, n % PR],
                                 start=(c == 0), stop=(c == NC - 1))
                last.then_inc(pv_done, 1)

            def project(b):
                pe.wait_ge(at_ready, 2 * b + 2)
                if b >= 1:
                    pe.wait_ge(rwt_ready, b)
                for t in range(NT):
                    last = pe.matmul(post[:, D * t:D * t + D], AT[:, P * t:P * t + P], WOG[:], start=True, stop=True)
                last.then_inc(o_done, 1)

            def t2(b):
                pe.wait_ge(xn2_ready, NT * (b + 1))
                for t in range(NT):
                    last = pe.transpose(post[:, P * t:P * t + P], XN2[:, t], ID[:])
                last.then_inc(t2_done, 1)

            def logits(b):
                pe.wait_ge(x2l_ready, b + 1)
                if b == 0:
                    pe.wait_ge(wffn_ready, 3)
                for t in range(NT):
                    toks = slice(P * t, P * t + P)
                    at = 2 * E * t
                    pe.matmul(post[:, at:at + 2 * E], X2H[:, b, toks], WRX[:].rearrange("d m e -> d (m e)"), start=True, stop=False)
                    last = pe.matmul(post[:, at:at + E], X2L[:, b, toks], WRX[:, 0], start=False, stop=True)
                last.then_inc(lg_done, 1)

            def routing_rows(b):
                pe.wait_ge(rhl_ready, b + 1)
                bank = post if b < B - 1 else drained_bank(("rt",))
                for t in range(NT):
                    last = pe.transpose(bank[0:2 * E, P * t:P * t + P], RHL[:, b, t].rearrange("p m e -> p (m e)").bitcast(F32), ID[:])
                last.then_inc(rt_done if b < B - 1 else filled, 1)

            def split_product(bank, w, c, b, done):
                at = slice(P * c, P * c + P)
                for k, (wt, xt) in enumerate(((WGUH, X2H), (WGUH, X2L), (WGUL, X2H))):
                    last = pe.matmul(bank[:], wt[:, w, at], xt[:, b], start=(k == 0), stop=(k == 2))
                last.then_inc(done, 1)

            def gate_up(n):
                b, c = n // FC, CHUNK_ORDER[n % FC]
                if n < 2:
                    pe.wait_ge(exp_ready, CH * B - 1 + n)
                else:
                    pe.wait_ge(silu_ready, n - 1)
                split_product(sring[n % 2], 0, c, b, gate_done)
                split_product(drained_bank(("up", n)), 1, c, b, filled)
                if c < EC:
                    m = EC * b + c
                    pe.wait_ge(at_ready, 2 * B)
                    if m >= 2:
                        pe.wait_ge(ar_ready, m - 1)
                    if b < B - 1:
                        pe.wait_ge(rwt_ready, b + 1)
                    else:
                        pe.wait_ge(drained, DRAIN[("rt",)] + 1)
                    pe.matmul(acc[c % 2][:], SELE[:, 2 * c:2 * c + 2].rearrange("p e f -> p (e f)"), RWT[:, b], start=True, stop=True).then_inc(rw_done, 1)

            def down(n):
                b, k = n // FC, n % FC
                c = CHUNK_ORDER[k]
                bank = (pre, post)[b % 2]
                pe.wait_ge(drained, DRAIN[("up", n)] + 1)
                if k == 0 and b == 0:
                    pe.wait_ge(wffn_ready, 5)
                if k == 0 and b == 1:
                    pe.wait_ge(lg_ready, B)
                if k == 0 and b >= 2:
                    pe.wait_ge(out_ready, b - 1)
                for t in range(NT):
                    last = pe.matmul(bank[:, D * t:D * t + D], HID[:, n % HR, P * t:P * t + P], WDG[:, c],
                                     start=(k == 0 and t == 0), stop=(k == FC - 1 and t == NT - 1), skip_group_check=True)
                last.then_inc(y_done if k == FC - 1 else y_chunk, 1)

            pe.wait_ge(const_ready, CONST_ID)
            pe.wait_ge(d_wq, 32)
            t1(0)
            q(0)
            pe.wait_ge(d_ctx, 32)
            pe.wait_ge(prep, PREP_MI)
            for b in range(B):
                context(b)
            t1(1)
            q(1)
            keys_k(0)
            pe.wait_ge(d_wv, 16)
            keys_v(0)
            for i in range(3):
                keys_vr(0, i)
            keys_k(1)
            keys_v(1)
            for i in range(3):
                keys_vr(1, i)
            pe.wait_ge(prep, PREP_BVB)
            pe.matmul(post[:, 0:D], BVB[:], WOG[:], start=True, stop=True).then_inc(bo_done, 1)
            for n in range(3 * NT):
                if n == 0:
                    pe.wait_ge(kx_ready, HG)
                    pe.wait_ge(d_q[0], 16 * TERMS * G)
                maximum(0, n)
            max_rows(0)
            pe.wait_ge(ind_ready, QB)
            pe.wait_ge(const_ready, CONST_PAD)
            for b in range(B):
                pe.wait_ge(d_m[b], 16 * G)
                for i in range(CH + LAG):
                    if i < CH:
                        scores(b, i)
                    if b + 1 < B:
                        if i == 0:
                            pe.wait_ge(kx_ready, HG * (b + 2))
                            pe.wait_ge(d_q[b + 1], 16 * TERMS * G)
                        for n in max_steps(i):
                            maximum(b + 1, n)
                    if i == 0 and b + 2 < B:
                        t1(b + 2)
                    if i == 1 and b + 2 < B:
                        q(b + 2)
                    if i == 3 and b >= 1:
                        if b == 1:
                            pe.wait_ge(bias_ready, 1)
                        project(b - 1)
                    if i == 6 and b >= 1:
                        t2(b - 1)
                    if i == 8 and b + 1 < B:
                        max_rows(b + 1)
                    if i == 8 and b + 2 < B:
                        keys_k(b + 2)
                    if i == 8 and b + 2 < B:
                        keys_v(b + 2)
                    if i == 8 and b >= 1:
                        logits(b - 1)
                    if i >= 9 and b + 2 < B:
                        keys_vr(b + 2, i - 9)
                    if i == 11 and b >= 1:
                        routing_rows(b - 1)
                    if i >= LAG:
                        weigh(b, i - LAG)
            pe.wait_ge(wffn_ready, 4)
            for n in range(FC * B + LAG):
                if n < FC * B:
                    gate_up(n)
                if n == 0:
                    project(B - 1)
                if n == 3:
                    t2(B - 1)
                if n == 4:
                    logits(B - 1)
                if n == LAST_ROUTE - 1:
                    routing_rows(B - 1)
                if n >= LAG:
                    down(n - LAG)


def kernel(**inputs):
    import numpy as np
    import concourse.bacc as bacc
    from concourse.bass_utils import run_bass_kernel_spmd

    names = ["x", "ctx_1024", "mask_BxS2_bk0", "g_xattn", "g_ffn",
             "L0_xattn_W_Q", "L0_xattn_b_Q", "L0_xattn_W_K", "L0_xattn_b_K", "L0_xattn_W_V", "L0_xattn_b_V",
             "L0_xattn_W_O", "L0_xattn_b_O", "L0_ffn_Wr", "L0_ffn_Wg", "L0_ffn_Wu", "L0_ffn_Wd",
             "L0_ffn_Sg", "L0_ffn_Su", "L0_ffn_Sd", "L0_ffn_expert_bias"]
    nc = bacc.Bacc("TRN2", target_bir_lowering=False, num_devices=1)
    arrays, args = {}, []
    for name in names:
        a = np.ascontiguousarray(inputs[name])
        if name == "L0_xattn_b_K":
            a = np.ascontiguousarray(a.reshape(G, GR).T)
        arrays[f"in_{name}"] = a
        args.append(nc.dram_tensor(f"in_{name}", a.shape, mybir.dt.from_np(a.dtype), kind="ExternalInput").ap())
    result = nc.dram_tensor("out_0", (B, S, D), F32, kind="ExternalOutput").ap()
    build(nc, *args, result)
    return run_bass_kernel_spmd(nc, [arrays], core_ids=[0]).results[0]["out_0"]
```

```python
from contextlib import ExitStack

import concourse.bass as bass
from concourse import mybir

F32 = mybir.dt.float32
F32R = mybir.dt.float32r
U8 = mybir.dt.uint8
ALU = mybir.AluOpType
ACT = mybir.ActivationFunctionType
AX = mybir.AxisListType

P = 128
B = 4
S = 512
D = 128
NT = S // P
H = 16
DH = D // H
LK = 77
G = 4
HG = H // G
GR = HG * DH
TERMS = 3
KR = TERMS * GR
MR = 2 * HG
GK = HG * LK
HALF = 2 * GK
NC = 5
CH = 2 * NC
GS = 436
E = 8
FE = 64
EC = E * FE // P
FC = EC + 1
EPS = 1e-5
QB = 3
PR = 4
HR = 4
LAG = 2
CHUNKS = CH * B
FFN = FC * B
MAX_RUN = [2, 2, 2, 2, 2, 1, 1]
MAXJ = [(0, 6), (6, 12), (12, 16)]


def chunk_rows(c):
    return min(P, HALF - P * c)


def kx_parts(half, c):
    parts = []
    if P * c < GK:
        parts.append((2 * half, 2 * half * GS + P * c))
    if P * c + chunk_rows(c) > GK:
        parts.append((2 * half + 1, 2 * half * GS + P + P * c))
    return parts


STEP = {
    "ln1_stats": [None, None, 0, 6], "ln1_apply": [None, None, 1, 8],
    "t1": [None, None, 2, 12], "xnt": [None, None, 1, 12], "q": [None, None, 3, 14],
    "qh": [None, None, 2, 12], "ql": [None, None, 4, 14],
    "k": [None, None, 4, 14], "kx": [None, None, 4, 14], "v": [None, 3, 5, 14], "vr": [1, 5, 8, 16],
    "mx": [None, 0, 9, 20], "split_max": [None, 6, 16, 26], "mt": [None, 7, 17, 27],
    "inverse0": [9, 16, 25, 37], "normalise0": [10, 18, 27, 39], "inverse1": [12, 22, 31, None], "normalise1": [14, 24, 33, None],
    "last_normalise": [41, 42],
    "project": [15, 24, 34, 47], "residual": [15, 25, 35, 47], "ln2": [17, 27, 36, 48], "t2": [18, 28, 39, 49],
    "x2h": [17, 27, 38, 49], "x2l": [18, 28, 39, 49], "logits": [19, 29, 41, 50], "sum": [19, 30, 41, 49], "first_pick": [20, 31, 44, 49], "pick": [22, 32, 45, 50],
    "weights": [24, 34, 46, 52], "rt": [27, 35, 48, 54],
    "wo": [0], "bo": [1], "bias": [6],
}


def due(stage, step):
    return [b for b, at in enumerate(STEP[stage]) if at == step]


def max_due(step):
    return [(b, n) for b in range(B) if STEP["mx"][b] is not None and 0 <= step - STEP["mx"][b] < len(MAX_RUN)
            for n in range(sum(MAX_RUN[:step - STEP["mx"][b]]), sum(MAX_RUN[:step - STEP["mx"][b] + 1]))]


def repeats_due(step):
    return [(b, i) for b in range(B) for i in range(3) if STEP["vr"][b] is not None and STEP["vr"][b] + i == step]


def drain_order():
    order = [("k", 0), ("k", 1), ("v", 0)] + [("mx", 0, n) for n in range(3 * NT)] + [("mt", 0)]
    for step in range(CHUNKS + FFN):
        if step >= CHUNKS:
            order.append(("up", step - CHUNKS))
        order += [("mx", b, n) for b, n in max_due(step)]
        for stage in ("mt", "k", "v"):
            order += [(stage, b) for b in due(stage, step)]
        order += [("vr", b, i) for b, i in repeats_due(step)]
        order += [("rt", b) for b in due("rt", step)]
    return order


DRAIN = {use: n for n, use in enumerate(drain_order())}


def ffn_chunk(n):
    b, k = n // FC, n % FC
    return b, (k - 1) % FC if b < B - 1 else k


def build(nc, x, ctx, mask, mask_t, g_att, g_ffn, w_q, b_q, b_qx, w_k, b_k, w_v, b_v, w_o, b_o,
          w_r, w_g, w_u, w_d, s_g, s_u, s_d, e_bias, out):
    with ExitStack() as stack:
        def sb(name, shape, dt=F32):
            return stack.enter_context(nc.sbuf_tensor(name, shape, dt))

        def ps(name):
            return stack.enter_context(nc.psum_tensor(name, [P, 512], F32))

        def sem(name):
            return stack.enter_context(nc.semaphore(name))

        X = sb("X", [P, B, NT, D])
        XR = sb("XR", [P, B, NT, D])
        CTX = sb("CTX", [LK, B, D])
        MASK8 = sb("MASK8", [LK, B, LK], U8); MASKT = sb("MASKT", [LK, B], U8)
        WQ = sb("WQ", [D, D]); WK = sb("WK", [D, D]); WV = sb("WV", [D, D]); WO = sb("WO", [D, D])
        BQ = sb("BQ", [D, 1]); BV = sb("BV", [D, 1]); BO = sb("BO", [P, D])
        BK = sb("BK", [KR, G]); BQX = sb("BQX", [KR, G])
        GATES = sb("GATES", [P, 2]); TG = sb("TG", [P, 2])
        WR = sb("WR", [D, E]); EB = sb("EB", [P, E])
        WGU = sb("WGU", [D, 2, FC * P])
        WD = sb("WD", [P, FC, D])
        ID = sb("ID", [P, P])
        NEG_HALF = sb("NEG_HALF", [P, NT]); EULER = sb("EULER", [P, NT])
        RANK = sb("RANK", [P, E])
        WKX = sb("WKX", [D, G, TERMS, GR])
        WOG = sb("WOG", [D, D])
        BVB = sb("BVB", [D, P])
        BIAS = sb("BIAS", [P, D])
        SEL = sb("SEL", [LK, 3, LK], F32R)
        BD = sb("BD", [P, NC, H // 2, DH])
        MK = sb("MK", [KR, HG])
        MI = sb("MI", [P, HG])
        MIH = sb("MIH", [2 * H, H])
        SELE0 = sb("SELE0", [2 * E, E])
        SELE = sb("SELE", [2 * E, E, FE], F32R)
        WGUH = sb("WGUH", [D, 2, FC * P], F32R); WGUL = sb("WGUL", [D, 2, FC * P], F32R)
        WRX = sb("WRX", [D, 2, E], F32R)
        WDG = sb("WDG", [P, FC, D])
        INV = sb("INV", [LK, B, LK]); RV = sb("RV", [LK, B])
        NV = sb("NV", [LK, B]); NV1 = sb("NV1", [LK, B]); RNV = sb("RNV", [LK, B])
        VC = sb("VC", [LK, B]); ALLM = sb("ALLM", [LK, B]); VE = sb("VE", [LK, B])
        AI = sb("AI", [LK, B, 2, LK])
        CT = sb("CT", [D, B, 2, LK])
        ST1 = sb("ST1", [P, B, NT, 6]); MV1 = sb("MV1", [P, B, NT, 2])
        VE1 = sb("VE1", [P, B, NT]); RS1 = sb("RS1", [P, B, NT])
        XN = sb("XN", [P, 2, NT, D]); XNT = sb("XNT", [D, 2, S])
        QH = sb("QH", [D, 2, S], F32R); QL = sb("QL", [D, 2, S], F32R)
        QX = sb("QX", [KR + MR, QB, G, S], F32R)
        KF = sb("KF", [KR, 2, G, LK]); KS = sb("KS", [KR, 2, G, LK], F32R)
        KX = sb("KX", [KR + MR, QB, G * GS], F32R)
        VF = sb("VF", [LK, 2, 2, D // 2])
        VRH = sb("VRH", [LK, 2, 4, D // 2], F32R); VRL = sb("VRL", [LK, 2, 2, D // 2], F32R)
        VBD = sb("VBD", [P, QB, NC, 2, P])
        MX = sb("MX", [P, B, NT, H])
        MHL = sb("MHL", [P, B, NT, G, 2, HG], F32R)
        MT = sb("MT", [2 * H, 2, S], F32R)
        PROB = sb("PROB", [P, PR, S])
        LD = sb("LD", [P, S]); RD = sb("RD", [P, S])
        AT = sb("AT", [D, S])
        ST2 = sb("ST2", [P, B, NT, 6]); MV2 = sb("MV2", [P, B, NT, 2])
        VE2 = sb("VE2", [P, B, NT]); RS2 = sb("RS2", [P, B, NT])
        XN2 = sb("XN2", [P, NT, D])
        X2H = sb("X2H", [D, B, S], F32R); X2L = sb("X2L", [D, B, S], F32R)
        WQX = PROB[:, 0, 0:TERMS * D].rearrange("p (g j r) -> p g j r", g=G, j=TERMS)
        IND = X2L[0:2 * H].rearrange("p b s -> p (b s)")[:, S:S + H * LK]
        LG = sb("LG", [P, B, NT, E]); LG2 = sb("LG2", [P, B, NT, E])
        EQ = sb("EQ", [P, B, 2, NT, E]); CA = sb("CA", [P, B, 2, NT, E]); OH = sb("OH", [P, B, 2, NT, E])
        M12 = sb("M12", [P, B, 2, NT]); RK = sb("RK", [P, B, 2, NT])
        DM = sb("DM", [P, B, NT]); EX = sb("EX", [P, B, NT]); SM = sb("SM", [P, B, NT])
        W1 = sb("W1", [P, B, NT]); W2 = sb("W2", [P, B, NT])
        RA = sb("RA", [P, B, NT, E]); RB = sb("RB", [P, B, NT, E]); RW = sb("RW", [P, B, NT, E])
        RHL = sb("RHL", [P, B, NT, 2, E], F32R)
        RWT = sb("RWT", [2 * E, B, S], F32R)
        AR = sb("AR", [P, 2, S])
        SL, HID, OUT = XNT, PROB, XN

        dring = [ps("dring0"), ps("dring1")]
        sring = [ps("sring0"), ps("sring1")]
        acc = [ps("acc0"), ps("acc1")]
        pre = ps("pre")
        post = ps("post")
        rw_bank, y_bank = acc[0], [pre, acc[1]]

        d_x = [sem(f"d_x{b}") for b in range(B)]
        d_mask = sem("d_mask"); d_ctx = sem("d_ctx"); d_att = sem("d_att"); d_ffn = sem("d_ffn")
        d_wq = sem("d_wq"); d_wk = sem("d_wk"); d_wv = sem("d_wv"); d_gate = sem("d_gate"); d_bq = sem("d_bq"); d_bq1 = sem("d_bq1")
        d_bk = sem("d_bk")
        d_q = [sem(f"d_q{b}") for b in range(B)]
        d_m = [sem(f"d_m{b}") for b in range(B)]
        d_out = [sem(f"d_out{b}") for b in range(B)]
        pool_step = sem("pool_step")
        const_ready = sem("const_ready")
        xb_ready = sem("xb_ready"); rs1_ready = sem("rs1_ready"); rs2_ready = sem("rs2_ready")
        ex_ready = sem("ex_ready"); wffn_ready = sem("wffn_ready")
        dve = sem("dve")
        prep = sem("prep")
        var1_ready = sem("var1_ready"); xn_ready = sem("xn_ready"); ql_ready = sem("ql_ready")
        ct_ready = sem("ct_ready"); ks_ready = sem("ks_ready"); vr_ready = sem("vr_ready")
        mhl_ready = sem("mhl_ready")
        bias_ready = sem("bias_ready")
        drained = sem("drained")
        at_ready = sem("at_ready"); x1_ready = sem("x1_ready"); var2_ready = sem("var2_ready")
        xn2_ready = sem("xn2_ready"); x2l_ready = sem("x2l_ready"); lg_ready = sem("lg_ready")
        dm_ready = sem("dm_ready"); rhl_ready = sem("rhl_ready")
        ar_ready = sem("ar_ready"); out_ready = sem("out_ready")
        wqx_ready = sem("wqx_ready"); q0h_ready = sem("q0h_ready"); q0l_ready = sem("q0l_ready")
        ct_done = sem("ct_done"); q0_done = sem("q0_done")
        tanh_ready = sem("tanh_ready"); ind_ready = sem("ind_ready")
        xnt_ready = sem("xnt_ready"); qh_ready = sem("qh_ready"); kx_ready = sem("kx_ready")
        exp_ready = sem("exp_ready"); ln_ready = sem("ln_ready"); rd_ready = sem("rd_ready")
        x2h_ready = sem("x2h_ready"); silu_ready = sem("silu_ready")
        filled = sem("filled")
        t1_done = sem("t1_done"); q_done = sem("q_done"); bo_done = sem("bo_done")
        s_done = sem("s_done"); pv_done = sem("pv_done");
        o_done = sem("o_done"); t2_done = sem("t2_done"); lg_done = sem("lg_done");
        gate_done = sem("gate_done"); rw_done = sem("rw_done"); y_chunk = sem("y_chunk"); y_done = sem("y_done")
        last_hidden = sem("last_hidden")

        PREP_MK, PREP_MI, PREP_MIH, PREP_SELE0, PREP_SEL, PREP_SELE, PREP_AI, PREP_AI2, PREP_WO, PREP_BVB = range(1, 11)
        CONST_ID, CONST_PAD, CONST_BD, CONST_RANK = 1, 2, 4, 5

        Q0_BANK = [sring[0], sring[1], acc[0], acc[1]]

        block = stack.enter_context(nc.Block())

        def tok(ap, b):
            return ap.rearrange("b (p t) d -> b p t d", t=NT)[b]

        def col(ap):
            return ap.rearrange("(p o) -> p o", o=1)

        def on_all(ap, n):
            return ap.rearrange("(o k) -> o k", o=1).to_broadcast([n, ap.shape[0]])

        @block.sync
        def _(sp):
            sp.dma_start(X[:, 0], tok(x, 0)).then_inc(d_x[0], 16)
            sp.dma_start(MASK8[:], mask.rearrange("(o b) k -> o b k", o=1).to_broadcast([LK, B, LK])).then_inc(d_mask, 16)
            sp.dma_start(MASKT[:], mask_t).then_inc(d_mask, 16)
            sp.dma_start(CTX[:], ctx.rearrange("b k d -> k b d")).then_inc(d_ctx, 16)
            sp.dma_start(X[:, 1], tok(x, 1)).then_inc(d_x[1], 16)
            sp.dma_start(WV[:], w_v).then_inc(d_wv, 16)
            sp.dma_start(BQ[:], col(b_q)).then_inc(d_bq1, 16)
            sp.dma_start(X[:, 2], tok(x, 2)).then_inc(d_x[2], 16)
            sp.dma_start(X[:, 3], tok(x, 3)).then_inc(d_x[3], 16)

            def send_q(b):
                if b >= QB:
                    sp.wait_ge(s_done, CH * (b - QB + 1))
                sp.wait_ge(qh_ready, b)
                for term, src in enumerate((QH, QH, QL)):
                    if src is QL:
                        sp.wait_ge(ql_ready, b)
                    for g in range(G):
                        rows = slice(GR * g, GR * g + GR)
                        sp.dma_start(QX[GR * term:GR * term + GR, b % QB, g, :].bitcast(F32),
                                     src[rows, b % 2, :].bitcast(F32)).then_inc(d_q[b], 16)

            def send_max(b):
                if b >= QB:
                    sp.wait_ge(s_done, CH * (b - QB + 1))
                sp.wait_ge(drained, DRAIN[("mt", b)] + 1)
                for g in range(G):
                    sp.dma_start(QX[KR:KR + MR, b % QB, g, :].bitcast(F32),
                                 MT[MR * g:MR * g + MR, b % 2, :].bitcast(F32)).then_inc(d_m[b], 16)

            sp.dma_start(WGU[:, 0, 0:EC * P].rearrange("d (e f) -> d e f", e=E), w_g.rearrange("e d f -> d e f")).then_inc(d_ffn, 16)
            sp.dma_start(WGU[:, 1, 0:EC * P].rearrange("d (e f) -> d e f", e=E), w_u.rearrange("e d f -> d e f")).then_inc(d_ffn, 16)
            sp.dma_start(WGU[:, 0, EC * P:], s_g).then_inc(d_ffn, 16)
            sp.dma_start(WGU[:, 1, EC * P:], s_u).then_inc(d_ffn, 16)
            sp.dma_start(WD[:, 0:EC, :], w_d.rearrange("(c e) f d -> (e f) c d", c=EC)).then_inc(d_ffn, 16)
            sp.dma_start(WD[:, EC, :], s_d).then_inc(d_ffn, 16)
            sp.dma_start(WR[:], w_r).then_inc(d_ffn, 16)
            send_q(1)
            for now in range(CHUNKS):
                for b in due("q", now):
                    send_q(b)
                for b in due("mt", now):
                    send_max(b)
            for b in range(B - 1):
                sp.wait_ge(out_ready, b + 1)
                sp.dma_start(tok(out, b), OUT[:, b % 2]).then_inc(d_out[b], 16)
            for half in range(2):
                tiles = slice(NT // 2 * half, NT // 2 * (half + 1))
                sp.wait_ge(out_ready, B + half)
                sp.dma_start(tok(out, B - 1)[:, tiles], OUT[:, (B - 1) % 2, tiles]).then_inc(d_out[B - 1], 16)
            for b in range(B):
                sp.wait_ge(d_out[b], 32 if b == B - 1 else 16)

        @block.gpsimd
        def _(pool):
            steps = [0]

            def step(ins):
                steps[0] += 1
                ins.then_inc(pool_step, 1)
                pool.wait_ge(pool_step, steps[0])

            step(pool.memset(ID[:], 0.0))
            pool.affine_select(out=ID[:], in_=ID[:], compare_op=ALU.not_equal, fill=1.0, base=0,
                               pattern=[[-1, P]], channel_multiplier=1).then_inc(const_ready, 1)
            step(pool.memset(NEG_HALF[:], -0.5))
            step(pool.memset(EULER[:], 2.718281828459045))
            for term in range(TERMS):
                pool.dma_start(BK[GR * term:GR * term + GR, :], b_k).then_inc(d_bk, 16)

            def rstd(mv, ve, rs, b, ready):
                step(pool.tensor_scalar(ve[:, b], mv[:, b, :, 1], EPS, None, ALU.add))
                pool.tensor_tensor(rs[:, b], ve[:, b], NEG_HALF[:], ALU.pow).then_inc(ready, 1)

            pool.wait_ge(var1_ready, 1)
            rstd(MV1, VE1, RS1, 0, rs1_ready)
            pad = KX[:].rearrange("p s (g c) -> p (s g) c", g=G)[:, :, GK:GS]
            pool.memset(pad.bitcast(F32), 0.0).then_inc(const_ready, 1)
            pool.wait_ge(var1_ready, 2)
            rstd(MV1, VE1, RS1, 1, rs1_ready)
            step(pool.memset(BD[:], 1.0))
            step(pool.affine_select(out=BD[:], in_=BD[:], compare_op=ALU.is_ge, fill=0.0, base=0,
                                    pattern=[[P, NC], [-LK, H // 2], [0, DH]], channel_multiplier=1))
            pool.affine_select(out=BD[:], in_=BD[:], compare_op=ALU.is_ge, fill=0.0, base=LK - 1,
                               pattern=[[-P, NC], [LK, H // 2], [0, DH]], channel_multiplier=-1).then_inc(const_ready, 2)
            pool.dma_start(GATES[:, 0:1], on_all(g_att, P)).then_inc(d_gate, 16)
            pool.dma_start(GATES[:, 1:2], on_all(g_ffn, P)).then_inc(d_gate, 16)
            pool.dma_start(WO[:], w_o).then_inc(d_att, 16)
            pool.dma_start(BV[:], col(b_v)).then_inc(d_att, 16)
            pool.dma_start(BO[:], on_all(b_o, P)).then_inc(d_att, 16)
            pool.dma_start(EB[:], on_all(e_bias, P)).then_inc(d_att, 16)
            for e in range(E):
                last = pool.memset(RANK[:, e:e + 1], float(E - e))
                if e < E - 1:
                    step(last)
            last.then_inc(const_ready, 1)

            def residual_bias(b):
                pool.wait_ge(d_x[b], 16)
                pool.wait_ge(bias_ready, 1)
                pool.tensor_tensor(XR[:, b], X[:, b], BIAS[:].unsqueeze(1).to_broadcast([P, NT, D]), ALU.add).then_inc(xb_ready, 1)

            pool.wait_ge(d_ffn, 16 * 7)
            pool.tensor_copy(WGUH[:], WGU[:]).then_inc(wffn_ready, 1)
            pool.tensor_copy(WRX[:, 0], WR[:]).then_inc(wffn_ready, 1)
            pool.wait_ge(wffn_ready, 2)
            pool.tensor_tensor(WRX[:, 1], WR[:], WRX[:, 0].bitcast(F32), ALU.subtract).then_inc(wffn_ready, 1)
            pool.tensor_tensor(WGUL[:], WGU[:], WGUH[:].bitcast(F32), ALU.subtract).then_inc(wffn_ready, 1)
            pool.wait_ge(tanh_ready, 1)
            pool.tensor_scalar(WDG[:], WD[:], TG[:, 1:2], None, ALU.mult).then_inc(wffn_ready, 1)
            pool.wait_ge(var1_ready, 3)
            rstd(MV1, VE1, RS1, 2, rs1_ready)
            pool.wait_ge(var1_ready, 4)
            rstd(MV1, VE1, RS1, 3, rs1_ready)
            residual_bias(0)
            for now in range(CHUNKS + FFN):
                for b in due("project", now):
                    if b + 1 < B:
                        residual_bias(b + 1)
                for b in due("residual", now):
                    pool.wait_ge(var2_ready, b + 1)
                    rstd(MV2, VE2, RS2, b, rs2_ready)
                for b in due("pick", now):
                    pool.wait_ge(dm_ready, b + 1)
                    pool.tensor_tensor(EX[:, b], EULER[:], DM[:, b], ALU.pow).then_inc(ex_ready, 1)

        @block.scalar
        def _(act):
            nc.scalar.preload_act_table_set("natural_log_exp_and_others")
            act.dma_start(WQ[:], w_q).then_inc(d_wq, 16)
            act.dma_start(WK[:], w_k).then_inc(d_wk, 16)
            for term in range(TERMS):
                act.dma_start(BQX[GR * term:GR * term + GR, :], b_qx).then_inc(d_bq, 16)

            def repeated(wx, w):
                return act.activation(wx, w[:].rearrange("p (g r) -> p g r", g=G).unsqueeze(2).to_broadcast([D, G, TERMS, GR]), ACT.Copy)

            act.wait_ge(d_wq, 16)
            repeated(WQX, WQ).then_inc(wqx_ready, 1)
            act.wait_ge(d_wk, 16)
            repeated(WKX[:], WK).then_inc(wqx_ready, 1)

            def xnt(b):
                act.wait_ge(t1_done, b + 1)
                if b == 2:
                    act.wait_ge(q0_done, G)
                if b == 3:
                    act.wait_ge(q_done, 1)
                act.activation(XNT[:, b % 2], pre[:], ACT.Copy).then_inc(xnt_ready, 1)

            def qh(b):
                act.wait_ge(q_done, b)
                if b >= 3:
                    act.wait_ge(d_q[b - 2], 16 * TERMS * G)
                act.activation(QH[:, b % 2], pre[:], ACT.Identity, bias=BQ[:]).then_inc(qh_ready, 1)

            def first_context(pair):
                act.wait_ge(ct_done, pair + 1)
                act.activation(CT[:, 2 * pair:2 * pair + 2].rearrange("p b a k -> p (b a k)"), post[:, 0:4 * LK], ACT.Copy).then_inc(ct_ready, 1)

            def first_queries(g):
                act.wait_ge(q0_done, g + 1)
                act.activation(QX[0:KR, 0, g], Q0_BANK[g][0:KR, :], ACT.Identity, bias=BQX[:, g:g + 1]).then_inc(q0h_ready, 1)

            def indicator(s):
                act.activation(KX[KR:KR + MR, s].rearrange("p (g c) -> p g c", g=G)[:, :, 0:GK]
                               .rearrange("p g (h k) -> p g h k", h=HG),
                               MI[KR:KR + MR, :].unsqueeze(1).unsqueeze(3).to_broadcast([MR, G, HG, LK]),
                               ACT.Copy).then_inc(ind_ready, 1)

            def kx(b, heads=range(HG)):
                act.wait_ge(ks_ready, b + 1)
                if b >= QB:
                    act.wait_ge(s_done, CH * (b - QB + 1))
                for h in heads:
                    act.activation(KX[0:KR, b % QB].rearrange("p (g c) -> p g c", g=G)[:, :, LK * h:LK * h + LK],
                                   KS[:, b % 2].bitcast(F32), ACT.Copy, scale=MK[:, h:h + 1]).then_inc(kx_ready, 1)

            def exp(n):
                rows = chunk_rows(n % NC)
                act.wait_ge(s_done, n + 1)
                if n >= PR:
                    act.wait_ge(pv_done, n - PR + 1)
                act.activation(PROB[0:rows, n % PR], sring[n % 2][0:rows, :], ACT.Exp, scale=DH ** -0.5).then_inc(exp_ready, 1)

            def inverse(b, half):
                n = 2 * b + half
                num, den = (slice(0, 64), slice(64, P)) if half == 0 else (slice(64, P), slice(0, 64))
                act.wait_ge(pv_done, NC * (n + 1))
                act.activation(LD[num], acc[n % 2][den, :], ACT.Ln).then_inc(ln_ready, 1)
                act.wait_ge(ln_ready, n + 1)
                if n >= 2:
                    act.wait_ge(at_ready, n - 1)
                act.activation(RD[num], LD[num], ACT.Exp, scale=-1.0).then_inc(rd_ready, 1)

            def x2h(b):
                act.wait_ge(t2_done, b + 1)
                act.activation(X2H[:, b], post[:], ACT.Copy).then_inc(x2h_ready, 1)

            xnt(0)
            first_context(0)
            act.wait_ge(d_bq, 48)
            first_queries(0)
            first_queries(1)
            first_queries(2)
            first_queries(3)
            kx(0)
            xnt(1)
            act.wait_ge(d_bq1, 16)
            qh(1)
            kx(1)
            act.wait_ge(prep, PREP_MIH)
            act.activation(IND.rearrange("p (h k) -> p h k", h=H), MIH[:].unsqueeze(2).to_broadcast([2 * H, H, LK]), ACT.Copy).then_inc(ind_ready, 1)
            indicator(1)
            first_context(1)
            act.wait_ge(d_gate, 32)
            act.activation(TG[:], GATES[:], ACT.Tanh).then_inc(tanh_ready, 1)
            nc.scalar.preload_act_table_set("natural_log_exp_and_others")
            indicator(2)
            indicator(0)

            def silu(n):
                act.wait_ge(gate_done, n + 1)
                if n >= 2:
                    act.wait_ge(drained, DRAIN[("up", n - 2)] + 1)
                act.activation(SL[:, n % 2], sring[n % 2][:], ACT.Silu).then_inc(silu_ready, 1)

            for now in range(CHUNKS + FFN):
                if now < CHUNKS:
                    exp(now)
                else:
                    silu(now - CHUNKS)
                for half in range(2):
                    for b in due(f"inverse{half}", now):
                        inverse(b, half)
                for b in due("xnt", now):
                    xnt(b)
                for b in due("qh", now):
                    qh(b)
                for b in range(2, B):
                    if 0 <= now - STEP["kx"][b] < HG:
                        kx(b, [now - STEP["kx"][b]])
                for b in due("x2h", now):
                    x2h(b)

        @block.vector
        def _(v):
            steps = [0]

            def step(ins):
                steps[0] += 1
                ins.then_inc(dve, 1)
                v.wait_ge(dve, steps[0])

            def mark(ins):
                steps[0] += 1
                ins.then_inc(dve, 1)
                return steps[0]

            def stats(src, st, mv, b, ready):
                for t in range(NT):
                    m = mark(v.bn_stats(st[:, b, t], src[:, b, t]))
                v.wait_ge(dve, m)
                for t in range(NT):
                    last = v.bn_aggr(mv[:, b, t], st[:, b, t])
                    if t < NT - 1:
                        mark(last)
                last.then_inc(ready, 1)

            def ln1_stats(b):
                v.wait_ge(d_x[b], 16)
                stats(X, ST1, MV1, b, var1_ready)

            def ln1_apply(b):
                v.wait_ge(rs1_ready, b + 1)
                if b >= 2:
                    v.wait_ge(t1_done, b - 1)
                for t in range(NT):
                    v.tensor_scalar(XN[:, b % 2, t], X[:, b, t], MV1[:, b, t, 0:1], RS1[:, b, t:t + 1],
                                    ALU.subtract, ALU.mult).then_inc(xn_ready, 1)

            def ql(b):
                v.wait_ge(q_done, b)
                v.wait_ge(qh_ready, b)
                if b >= 3:
                    v.wait_ge(d_q[b - 2], 16 * TERMS * G)
                v.scalar_tensor_tensor(QL[:, b % 2], pre[:], BQ[:], QH[:, b % 2].bitcast(F32), ALU.add, ALU.subtract).then_inc(ql_ready, 1)

            def first_queries(g):
                lo = slice(2 * GR, KR)
                v.wait_ge(q0h_ready, g + 1)
                v.scalar_tensor_tensor(QX[lo, 0, g], Q0_BANK[g][lo, :], BQX[lo, g:g + 1], QX[lo, 0, g].bitcast(F32),
                                       ALU.add, ALU.subtract).then_inc(q0l_ready, 1)

            def full(use):
                v.wait_ge(filled, DRAIN[use] + 1)
                return dring[DRAIN[use] % 2]

            def keys_k(b):
                bank = full(("k", b))
                v.tensor_tensor(KF[:, b % 2], bank[0:KR, 0:GK].rearrange("p (g k) -> p g k", g=G),
                                BK[:].unsqueeze(2).to_broadcast([KR, G, LK]), ALU.add).then_inc(drained, 1)
                v.wait_ge(drained, DRAIN[("k", b)] + 1)
                if b >= 2:
                    v.wait_ge(kx_ready, HG * (b - 1))
                step(v.tensor_copy(KS[:, b % 2], KF[:, b % 2]))
                lo = slice(GR, 2 * GR)
                v.tensor_tensor(KS[lo, b % 2], KF[lo, b % 2], KS[lo, b % 2].bitcast(F32), ALU.subtract).then_inc(ks_ready, 1)

            def keys_v(b):
                bank = full(("v", b))
                v.tensor_scalar(VF[:, b % 2], bank[0:LK, 0:D].rearrange("p (a c) -> p a c", a=2), VE[:, b:b + 1], None, ALU.mult).then_inc(drained, 1)
                v.wait_ge(drained, DRAIN[("v", b)] + 1)
                if b >= 2:
                    v.wait_ge(filled, DRAIN[("vr", b - 2, 2)] + 1)
                mark(v.tensor_copy(VRH[:, b % 2, 0:4:3], VF[:, b % 2]))
                step(v.tensor_copy(VRH[:, b % 2, 1:3], VE[:, b:b + 1].unsqueeze(2).to_broadcast([LK, 2, D // 2])))
                v.tensor_tensor(VRL[:, b % 2], VF[:, b % 2], VRH[:, b % 2, 0:4:3].bitcast(F32), ALU.subtract).then_inc(vr_ready, 1)

            def keys_vr(b, i):
                bank = full(("vr", b, i))
                first, last = 2 * i, min(2 * i + 2, NC)
                if i == 0 and b >= QB:
                    v.wait_ge(pv_done, CH * (b - QB + 1))
                v.tensor_tensor(VBD[:, b % QB, first:last].rearrange("p c a (t n) -> p c (a t) n", t=2),
                                bank[:, 0:(last - first) * 2 * P].rearrange("p (c q n) -> p c q n", q=4, n=P // 2),
                                BD[:, first:last].rearrange("p c h d -> p c (h d)").unsqueeze(2).to_broadcast([P, last - first, 4, P // 2]),
                                ALU.mult).then_inc(drained, 1)

            def maximum(b, n):
                bank = full(("mx", b, n))
                h0, h1 = MAXJ[n % 3]
                v.tensor_reduce(MX[:, b, n // 3, h0:h1], bank[:, 0:(h1 - h0) * LK].rearrange("p (h k) -> p h k", k=LK), AX.X, ALU.max).then_inc(drained, 1)

            def split_max(b):
                v.wait_ge(drained, DRAIN[("mx", b, 3 * NT - 1)] + 1)
                mx = MX[:, b].rearrange("p t (g r) -> p (t g) r", g=G)
                hl = MHL[:, b].rearrange("p t g m r -> p (t g) m r")
                step(v.tensor_scalar(hl[:, :, 0, :], mx, -1.0, None, ALU.mult))
                v.scalar_tensor_tensor(hl[:, :, 1, :], mx, -1.0, hl[:, :, 0, :].bitcast(F32), ALU.mult, ALU.subtract).then_inc(mhl_ready, 1)

            def max_rows(b):
                bank = full(("mt", b))
                if b == 2:
                    v.wait_ge(s_done, CH)
                if b == 3:
                    v.wait_ge(d_m[1], 16 * G)
                v.tensor_copy(MT[:, b % 2], bank[0:2 * H, :]).then_inc(drained, 1)

            def normalise(b, half):
                n = 2 * b + half
                num = slice(0, 64) if half == 0 else slice(64, P)
                v.wait_ge(rd_ready, n + 1)
                if b >= 1:
                    v.wait_ge(o_done, b)
                v.tensor_tensor(AT[num], acc[n % 2][num, :], RD[num], ALU.mult).then_inc(at_ready, 1)

            def last_normalise(part):
                n = 2 * B - 1
                num, den, toks = slice(64, P), slice(0, 64), slice(S // 2 * part, S // 2 * (part + 1))
                v.wait_ge(pv_done, NC * (n + 1))
                v.wait_ge(at_ready, n - 1)
                step(v.reciprocal(RD[num, toks], acc[n % 2][den, toks]))
                v.wait_ge(o_done, B - 1)
                last = v.tensor_tensor(AT[num, toks], acc[n % 2][num, toks], RD[num, toks], ALU.mult)
                if part == 0:
                    mark(last)
                else:
                    last.then_inc(at_ready, 1)

            def residual(b):
                v.wait_ge(o_done, b + 1)
                v.wait_ge(xb_ready, b + 1)
                v.tensor_tensor(XR[:, b].rearrange("p t d -> p (t d)"), post[:], XR[:, b].rearrange("p t d -> p (t d)"), ALU.add).then_inc(x1_ready, 1)
                v.wait_ge(x1_ready, b + 1)
                stats(XR, ST2, MV2, b, var2_ready)

            def ln2_apply(b):
                v.wait_ge(rs2_ready, b + 1)
                if b >= 1:
                    v.wait_ge(t2_done, b)
                for t in range(NT):
                    v.tensor_scalar(XN2[:, t], XR[:, b, t], MV2[:, b, t, 0:1], RS2[:, b, t:t + 1],
                                    ALU.subtract, ALU.mult).then_inc(xn2_ready, 1)

            def x2l(b):
                v.wait_ge(x2h_ready, b + 1)
                v.tensor_tensor(X2L[:, b], post[:], X2H[:, b].bitcast(F32), ALU.subtract).then_inc(x2l_ready, 1)

            def over_experts(a):
                return a.unsqueeze(2).to_broadcast([P, NT, E])

            def over_tiles(a):
                return a.unsqueeze(1).to_broadcast([P, NT, E])

            def pick(b, k, logits):
                step(v.tensor_reduce(M12[:, b, k], logits, AX.X, ALU.max))
                step(v.tensor_tensor(EQ[:, b, k], logits, over_experts(M12[:, b, k]), ALU.is_equal))
                step(v.tensor_tensor(CA[:, b, k], EQ[:, b, k], over_tiles(RANK[:]), ALU.mult))
                step(v.tensor_reduce(RK[:, b, k], CA[:, b, k], AX.X, ALU.max))
                step(v.tensor_tensor(OH[:, b, k], over_tiles(RANK[:]), over_experts(RK[:, b, k]), ALU.is_equal))

            def logit_sum(b):
                v.wait_ge(lg_done, b + 1)
                v.tensor_reduce(LG2[:, b], post[:, 0:NT * 2 * E].rearrange("p (t m e) -> p t e m", t=NT, m=2), AX.X, ALU.add).then_inc(lg_ready, 1)

            def first_pick(b):
                v.wait_ge(lg_ready, b + 1)
                v.wait_ge(const_ready, CONST_RANK)
                step(v.tensor_tensor(LG[:, b], LG2[:, b], over_tiles(EB[:]), ALU.add))
                pick(b, 0, LG[:, b])
                step(v.scalar_tensor_tensor(LG2[:, b], OH[:, b, 0], -3.0e38, LG[:, b], ALU.mult, ALU.add))

            def second_pick(b):
                pick(b, 1, LG2[:, b])
                v.tensor_tensor(DM[:, b], M12[:, b, 1], M12[:, b, 0], ALU.subtract).then_inc(dm_ready, 1)

            def route_weights(b):
                v.wait_ge(ex_ready, b + 1)
                step(v.tensor_scalar(SM[:, b], EX[:, b], 1.0, None, ALU.add))
                step(v.reciprocal(W1[:, b], SM[:, b]))
                step(v.tensor_tensor(W2[:, b], EX[:, b], W1[:, b], ALU.mult))
                mark(v.tensor_tensor(RA[:, b], OH[:, b, 0], over_experts(W1[:, b]), ALU.mult))
                step(v.tensor_tensor(RB[:, b], OH[:, b, 1], over_experts(W2[:, b]), ALU.mult))
                step(v.tensor_tensor(RW[:, b], RA[:, b], RB[:, b], ALU.add))
                step(v.tensor_copy(RHL[:, b, :, 0], RW[:, b]))
                v.tensor_tensor(RHL[:, b, :, 1], RW[:, b], RHL[:, b, :, 0].bitcast(F32), ALU.subtract).then_inc(rhl_ready, 1)

            def finish_rows(b):
                v.wait_ge(y_done, b + 1)
                if b >= 2:
                    v.wait_ge(d_out[b - 2], 16)
                bank = y_bank[b % 2]
                v.tensor_tensor(OUT[:, b % 2].rearrange("p t d -> p (t d)"), bank[:], XR[:, b].rearrange("p t d -> p (t d)"), ALU.add).then_inc(out_ready, 1)

            v.wait_ge(const_ready, CONST_ID)
            v.tensor_reduce(MK[:], ID[0:KR, 0:KR].rearrange("p (j h d) -> p h j d", j=TERMS, h=HG), AX.XY, ALU.add).then_inc(prep, 1)
            v.tensor_reduce(MI[KR:KR + MR], ID[KR:KR + MR, KR:KR + MR].rearrange("p (j h) -> p h j", h=HG), AX.X, ALU.add).then_inc(prep, 1)
            v.tensor_reduce(MIH[:].rearrange("p (g h) -> p g h", g=G), ID[0:2 * H, 0:2 * H].rearrange("p (g j h) -> p g h j", g=G, j=2), AX.X, ALU.add).then_inc(prep, 1)
            v.tensor_reduce(SELE0[:], ID[0:2 * E, 0:2 * E].rearrange("p (j e) -> p e j", j=2), AX.X, ALU.add).then_inc(prep, 1)
            v.tensor_copy(SEL[:], ID[0:LK, 0:LK].unsqueeze(1).to_broadcast([LK, 3, LK])).then_inc(prep, 1)
            v.wait_ge(prep, PREP_SELE0)
            v.tensor_copy(SELE[:], SELE0[:].unsqueeze(2).to_broadcast([2 * E, E, FE])).then_inc(prep, 1)
            ln1_stats(0)
            v.wait_ge(d_mask, 32)
            mark(v.tensor_scalar(VC[:], MASKT[:], -1.0, 1.0, ALU.mult, ALU.add))
            step(v.tensor_copy(INV[:], MASK8[:]))
            step(v.tensor_reduce(NV[:], INV[:], AX.X, ALU.add))
            step(v.tensor_scalar(NV1[:], NV[:], -1.0, float(LK), ALU.mult, ALU.add))
            ln1_apply(0)
            mark(v.tensor_scalar(ALLM[:], NV1[:], 0.0, None, ALU.is_equal))
            step(v.tensor_scalar(NV1[:], NV1[:], 1.0, None, ALU.max))
            ident = ID[0:LK, 0:LK].unsqueeze(1).to_broadcast([LK, B, LK])
            mark(v.tensor_copy(AI[:, :, 1], ident))
            step(v.reciprocal(RNV[:], NV1[:]))
            step(v.tensor_tensor(RV[:], RNV[:], VC[:], ALU.mult))
            def mixing(b0, b1):
                for b in range(b0, b1):
                    mark_a = mark(v.scalar_tensor_tensor(AI[:, b, 0], ID[0:LK, 0:LK], VC[:, b:b + 1], ID[0:LK, 0:LK], ALU.mult, ALU.mult))
                v.wait_ge(dve, mark_a)
                for b in range(b0, b1):
                    last = v.scalar_tensor_tensor(AI[:, b, 0], INV[:, b], RV[:, b:b + 1], AI[:, b, 0], ALU.mult, ALU.add)
                    if b < b1 - 1:
                        mark(last)
                last.then_inc(prep, 1)

            mixing(0, 2)
            ln1_stats(1)
            mixing(2, B)
            mark(v.tensor_tensor(VE[:], VC[:], ALLM[:], ALU.add))
            first_queries(0)
            ln1_apply(1)
            v.wait_ge(d_bk, 48)
            keys_k(0)
            for g in range(1, G):
                first_queries(g)
            keys_k(1)
            keys_v(0)
            for n in range(3 * NT):
                maximum(0, n)
                if n == 1:
                    ql(1)
            split_max(0)
            max_rows(0)
            v.wait_ge(const_ready, CONST_BD)

            def hidden(n):
                b, c = ffn_chunk(n)
                bank = full(("up", n))
                if n < HR:
                    v.wait_ge(pv_done, CHUNKS - HR + n + 1)
                elif (n - HR) % FC < FC - 1:
                    v.wait_ge(y_chunk, (n - HR) - (n - HR) // FC + 1)
                else:
                    v.wait_ge(y_done, (n - HR) // FC + 1)
                v.wait_ge(silu_ready, n + 1)
                if n == FFN - 1:
                    for at in (slice(0, S // 2), slice(S // 2, S)):
                        v.tensor_tensor(HID[:, n % HR, at], SL[:, n % 2, at], bank[:, at], ALU.mult).then_inc(last_hidden, 1)
                elif c == FC - 1:
                    v.tensor_tensor(HID[:, n % HR], SL[:, n % 2], bank[:], ALU.mult).then_inc(drained, 1)
                else:
                    v.wait_ge(rw_done, EC * b + c + 1)
                    v.tensor_tensor(AR[:, n % 2], SL[:, n % 2], rw_bank[:], ALU.mult).then_inc(ar_ready, 1)
                    v.wait_ge(ar_ready, EC * b + c + 1)
                    v.tensor_tensor(HID[:, n % HR], AR[:, n % 2], bank[:], ALU.mult).then_inc(drained, 1)

            for now in range(CHUNKS + FFN):
                if now >= CHUNKS:
                    hidden(now - CHUNKS)
                for half in range(2):
                    for b in due(f"normalise{half}", now):
                        normalise(b, half)
                for part in due("last_normalise", now):
                    last_normalise(part)
                for b, n in max_due(now):
                    maximum(b, n)
                for b in due("split_max", now):
                    split_max(b)
                for b in due("ql", now):
                    ql(b)
                for _ in due("wo", now):
                    v.wait_ge(tanh_ready, 1)
                    v.wait_ge(d_att, 64)
                    v.tensor_scalar(WOG[:], WO[:], TG[:, 0:1], None, ALU.mult).then_inc(prep, 1)
                    v.tensor_copy(BVB[:], BV[:].to_broadcast([D, P])).then_inc(prep, 1)
                for _ in due("bias", now):
                    v.wait_ge(bo_done, 1)
                    v.scalar_tensor_tensor(BIAS[:], BO[:], TG[:, 0:1], post[:, 0:D], ALU.mult, ALU.add).then_inc(bias_ready, 1)
                for b in due("mt", now):
                    max_rows(b)
                for b in due("k", now):
                    keys_k(b)
                for b in due("v", now):
                    keys_v(b)
                for b, i in repeats_due(now):
                    keys_vr(b, i)
                for b in due("residual", now):
                    residual(b)
                for b in due("ln2", now):
                    ln2_apply(b)
                for b in due("x2l", now):
                    x2l(b)
                for b in due("ln1_stats", now):
                    ln1_stats(b)
                for b in due("ln1_apply", now):
                    ln1_apply(b)
                for b in due("sum", now):
                    logit_sum(b)
                for b in due("first_pick", now):
                    first_pick(b)
                for b in due("pick", now):
                    second_pick(b)
                for b in due("weights", now):
                    route_weights(b)
                for b in due("rt", now):
                    v.tensor_copy(RWT[:, b], full(("rt", b))[0:2 * E, :]).then_inc(drained, 1)
                if now > CHUNKS + FC and (now - CHUNKS) % FC == LAG:
                    finish_rows((now - CHUNKS) // FC - 1)
            v.wait_ge(d_out[B - 3], 16)
            for half in range(2):
                v.wait_ge(y_done, B + half)
                tiles = slice(NT // 2 * half, NT // 2 * (half + 1))
                v.tensor_tensor(OUT[:, (B - 1) % 2, tiles], (y_bank[(B - 1) % 2], post)[half][:].rearrange("p (t d) -> p t d", t=NT)[:, tiles],
                                XR[:, B - 1, tiles], ALU.add).then_inc(out_ready, 1)

        @block.tensor
        def _(pe):
            def drained_bank(use):
                n = DRAIN[use]
                if n >= 2:
                    pe.wait_ge(drained, n - 1)
                return dring[n % 2]

            def t1(b):
                pe.wait_ge(xn_ready, NT * (b + 1))
                if b == 1:
                    pe.wait_ge(xnt_ready, 1)
                if b >= 2:
                    pe.wait_ge(qh_ready, b - 1)
                    pe.wait_ge(ql_ready, b - 1)
                for t in range(NT):
                    last = pe.transpose(pre[:, P * t:P * t + P], XN[:, b % 2, t], ID[:])
                last.then_inc(t1_done, 1)

            def q(b):
                pe.wait_ge(xnt_ready, b + 1)
                pe.matmul(pre[:], WQ[:], XNT[:, b % 2], start=True, stop=True).then_inc(q_done, 1)

            def context(pair):
                if pair > 0:
                    pe.wait_ge(ct_ready, pair)
                for b in (2 * pair, 2 * pair + 1):
                    at = 2 * LK * (b - 2 * pair)
                    last = pe.matmul(post[:, at:at + 2 * LK], CTX[:, b], AI[:, b].rearrange("p a k -> p (a k)"), start=True, stop=True)
                last.then_inc(ct_done, 1)

            def first_queries(g):
                pe.matmul(Q0_BANK[g][0:KR, :], WQX[:, g].rearrange("p j r -> p (j r)"), XNT[:, 0], start=True, stop=True).then_inc(q0_done, 1)

            def keys_k(b):
                bank = drained_bank(("k", b))
                pe.wait_ge(ct_ready, b // 2 + 1)
                for g in range(G):
                    last = pe.matmul(bank[0:KR, LK * g:LK * g + LK], WKX[:, g].rearrange("p a r -> p (a r)"), CT[:, b, 0],
                                     start=True, stop=True)
                last.then_inc(filled, 1)

            def keys_v(b):
                bank = drained_bank(("v", b))
                pe.matmul(bank[0:LK, 0:D], CT[:, b, 1], WV[:], start=True, stop=True).then_inc(filled, 1)

            def keys_vr(b, i):
                bank = drained_bank(("vr", b, i))
                pe.wait_ge(vr_ready, b + 1)
                sel = SEL[:].rearrange("p a k -> p (a k)")
                for c in range(2 * i, min(2 * i + 2, NC)):
                    at = P * c % LK
                    both = bank[:, 2 * P * (c - 2 * i):2 * P * (c - 2 * i + 1)]
                    pe.matmul(both, sel[:, at:at + P], VRH[:, b % 2].rearrange("p a n -> p (a n)"), start=True, stop=False)
                    last = pe.matmul(both.rearrange("p (q n) -> p q n", q=4)[:, 0:4:3], sel[:, at:at + P], VRL[:, b % 2],
                                     start=False, stop=True)
                last.then_inc(filled, 1)

            def maximum(b, n):
                bank = drained_bank(("mx", b, n))
                t = n // 3
                h0, h1 = MAXJ[n % 3]
                h = h0
                while h < h1:
                    g, end = h // HG, min(h1, (h // HG + 1) * HG)
                    at = GS * g + LK * (h - HG * g)
                    last = pe.matmul(bank[:, LK * (h - h0):LK * (end - h0)], QX[0:KR, b % QB, g, P * t:P * t + P],
                                     KX[0:KR, b % QB, at:at + LK * (end - h)], start=True, stop=True)
                    h = end
                last.then_inc(filled, 1)

            def max_rows(b):
                bank = drained_bank(("mt", b))
                pe.wait_ge(mhl_ready, b + 1)
                for t in range(NT):
                    last = pe.transpose(bank[0:2 * H, P * t:P * t + P], MHL[:, b, t].rearrange("p g m r -> p (g m r)").bitcast(F32), ID[:])
                last.then_inc(filled, 1)

            def scores(n):
                b, i = n // CH, n % CH
                half, c = i // NC, i % NC
                rows = chunk_rows(c)
                if n >= 2:
                    pe.wait_ge(exp_ready, n - 1)
                parts = kx_parts(half, c)
                depth = KR if b == 0 else KR + MR
                for k, (g, at) in enumerate(parts):
                    last = pe.matmul(sring[n % 2][0:rows, :], KX[0:depth, b % QB, at:at + rows], QX[0:depth, b % QB, g],
                                     start=(k == 0), stop=(b > 0 and k == len(parts) - 1))
                if b == 0:
                    at = half * HALF + P * c
                    last = pe.matmul(sring[n % 2][0:rows, :], IND[:, at:at + rows], MT[:, 0], start=False, stop=True)
                last.then_inc(s_done, 1)

            def weigh(n):
                b, i = n // CH, n % CH
                half, c = i // NC, i % NC
                rows = chunk_rows(c)
                if c == 0 and 2 * b + half >= 2:
                    pe.wait_ge(at_ready, 2 * b + half - 1)
                pe.wait_ge(exp_ready, n + 1)
                last = pe.matmul(acc[(2 * b + half) % 2][:], VBD[0:rows, b % QB, c, half], PROB[0:rows, n % PR],
                                 start=(c == 0), stop=(c == NC - 1))
                last.then_inc(pv_done, 1)

            def project(b):
                pe.wait_ge(at_ready, 2 * b + 2)
                pe.wait_ge(*((lg_ready, b) if b >= 1 else (bias_ready, 1)))
                for t in range(NT):
                    last = pe.matmul(post[:, D * t:D * t + D], AT[:, P * t:P * t + P], WOG[:], start=True, stop=True)
                last.then_inc(o_done, 1)

            def t2(b):
                pe.wait_ge(xn2_ready, NT * (b + 1))
                for t in range(NT):
                    last = pe.transpose(post[:, P * t:P * t + P], XN2[:, t], ID[:])
                last.then_inc(t2_done, 1)

            def logits(b):
                pe.wait_ge(x2l_ready, b + 1)
                if b == 0:
                    pe.wait_ge(wffn_ready, 3)
                for t in range(NT):
                    toks = slice(P * t, P * t + P)
                    at = 2 * E * t
                    pe.matmul(post[:, at:at + 2 * E], X2H[:, b, toks], WRX[:].rearrange("d m e -> d (m e)"), start=True, stop=False)
                    last = pe.matmul(post[:, at:at + E], X2L[:, b, toks], WRX[:, 0], start=False, stop=True)
                last.then_inc(lg_done, 1)

            def routing_rows(b):
                pe.wait_ge(rhl_ready, b + 1)
                bank = drained_bank(("rt", b))
                for t in range(NT):
                    last = pe.transpose(bank[0:2 * E, P * t:P * t + P], RHL[:, b, t].rearrange("p m e -> p (m e)").bitcast(F32), ID[:])
                last.then_inc(filled, 1)

            def split_product(bank, w, c, b, done):
                at = slice(P * c, P * c + P)
                for k, (wt, xt) in enumerate(((WGUH, X2H), (WGUH, X2L), (WGUL, X2H))):
                    last = pe.matmul(bank[:], wt[:, w, at], xt[:, b], start=(k == 0), stop=(k == 2))
                last.then_inc(done, 1)

            def gate_up(n):
                b, c = ffn_chunk(n)
                if n < 2:
                    pe.wait_ge(exp_ready, CH * B - 1 + n)
                else:
                    pe.wait_ge(silu_ready, n - 1)
                split_product(sring[n % 2], 0, c, b, gate_done)
                split_product(drained_bank(("up", n)), 1, c, b, filled)
                if c < EC:
                    m = EC * b + c
                    if m >= 1:
                        pe.wait_ge(ar_ready, m)
                    else:
                        pe.wait_ge(at_ready, 2 * B - 1)
                    pe.wait_ge(drained, DRAIN[("rt", b)] + 1)
                    pe.matmul(rw_bank[:], SELE[:, 2 * c:2 * c + 2].rearrange("p e f -> p (e f)"), RWT[:, b], start=True, stop=True).then_inc(rw_done, 1)

            def down(n):
                b, k = n // FC, n % FC
                b, c = ffn_chunk(n)
                bank = y_bank[b % 2]
                if n < FFN - 1:
                    pe.wait_ge(drained, DRAIN[("up", n)] + 1)
                if k == 0 and b == 0:
                    pe.wait_ge(wffn_ready, 5)
                if k == 0 and b == 1:
                    pe.wait_ge(at_ready, 2 * B)
                if k == 0 and b == B - 1:
                    pe.wait_ge(lg_ready, B)
                first, final = ((0,), (NT - 1,)) if b < B - 1 else ((0, NT // 2), (NT // 2 - 1, NT - 1))
                if k == 0 and b >= 2:
                    pe.wait_ge(out_ready, b - 1)
                for t in range(NT):
                    if n == FFN - 1 and t % (NT // 2) == 0:
                        pe.wait_ge(last_hidden, t // (NT // 2) + 1)
                    if b == B - 1 and t == NT // 2:
                        bank = post
                    last = pe.matmul(bank[:, D * t:D * t + D], HID[:, n % HR, P * t:P * t + P], WDG[:, c],
                                     start=(k == 0 and t in first), stop=(k == FC - 1 and t in final), skip_group_check=True)
                    if n == FFN - 1 and t == NT // 2 - 1:
                        last.then_inc(y_done, 1)
                last.then_inc(y_done if k == FC - 1 else y_chunk, 1)

            pe.wait_ge(const_ready, CONST_ID)
            t1(0)
            pe.wait_ge(d_ctx, 16)
            pe.wait_ge(prep, PREP_AI)
            context(0)
            pe.wait_ge(wqx_ready, 1)
            pe.wait_ge(xnt_ready, 1)
            first_queries(0)
            pe.wait_ge(wqx_ready, 2)
            keys_k(0)
            first_queries(1)
            first_queries(2)
            first_queries(3)
            keys_k(1)
            t1(1)
            pe.wait_ge(d_wv, 16)
            keys_v(0)
            pe.wait_ge(prep, PREP_AI2)
            context(1)
            q(1)
            pe.wait_ge(kx_ready, HG)
            pe.wait_ge(q0l_ready, G)
            for n in range(3 * NT):
                maximum(0, n)
            max_rows(0)
            pe.wait_ge(drained, DRAIN[("mt", 0)] + 1)
            pe.wait_ge(const_ready, CONST_PAD)
            for now in range(CHUNKS + FFN + LAG):
                if now < CHUNKS:
                    if now % CH == 0:
                        pe.wait_ge(ind_ready, now // CH + 1)
                        if now > 0:
                            pe.wait_ge(d_m[now // CH], 16 * G)
                    scores(now)
                elif now < CHUNKS + FFN:
                    if now == CHUNKS:
                        pe.wait_ge(wffn_ready, 4)
                    gate_up(now - CHUNKS)
                for b, n in max_due(now):
                    if n == 0:
                        pe.wait_ge(kx_ready, HG * (b + 1))
                        pe.wait_ge(d_q[b], 16 * TERMS * G)
                    maximum(b, n)
                for b in due("t1", now):
                    t1(b)
                for b in due("q", now):
                    q(b)
                for _ in due("bo", now):
                    pe.wait_ge(prep, PREP_BVB)
                    pe.wait_ge(ct_ready, 2)
                    pe.matmul(post[:, 0:D], BVB[:], WOG[:], start=True, stop=True).then_inc(bo_done, 1)
                for b in due("project", now):
                    project(b)
                for b in due("t2", now):
                    t2(b)
                for b in due("mt", now):
                    max_rows(b)
                for b in due("k", now):
                    keys_k(b)
                for b in due("v", now):
                    keys_v(b)
                for b in due("logits", now):
                    logits(b)
                for b, i in repeats_due(now):
                    keys_vr(b, i)
                for b in due("rt", now):
                    routing_rows(b)
                if LAG <= now < CHUNKS + LAG:
                    weigh(now - LAG)
                elif now >= CHUNKS + LAG:
                    down(now - CHUNKS - LAG)


def kernel(**inputs):
    import numpy as np
    import concourse.bacc as bacc
    from concourse.bass_utils import run_bass_kernel_spmd

    names = ["x", "ctx_1024", "mask_BxS2_bk0", "g_xattn", "g_ffn",
             "L0_xattn_W_Q", "L0_xattn_b_Q", "L0_xattn_W_K", "L0_xattn_b_K", "L0_xattn_W_V", "L0_xattn_b_V",
             "L0_xattn_W_O", "L0_xattn_b_O", "L0_ffn_Wr", "L0_ffn_Wg", "L0_ffn_Wu", "L0_ffn_Wd",
             "L0_ffn_Sg", "L0_ffn_Su", "L0_ffn_Sd", "L0_ffn_expert_bias"]
    nc = bacc.Bacc("TRN2", target_bir_lowering=False, num_devices=1)
    arrays, args = {}, []
    for name in names:
        a = np.ascontiguousarray(inputs[name])
        if name == "L0_xattn_b_K":
            a = np.ascontiguousarray(a.reshape(G, GR).T)
        views = [a]
        if name == "mask_BxS2_bk0":
            views.append(np.ascontiguousarray(a.T))
        if name == "L0_xattn_b_Q":
            views.append(np.ascontiguousarray(a.reshape(G, GR).T))
        for i, a in enumerate(views):
            arrays[f"in{i}_{name}"] = a
            args.append(nc.dram_tensor(f"in{i}_{name}", a.shape, mybir.dt.from_np(a.dtype), kind="ExternalInput").ap())
    result = nc.dram_tensor("out_0", (B, S, D), F32, kind="ExternalOutput").ap()
    build(nc, *args, result)
    return run_bass_kernel_spmd(nc, [arrays], core_ids=[0]).results[0]["out_0"]
```
